# Optimizing a Trainium2 kernel written in Bass

```python
import numpy as np
import jax
import jax.numpy as jnp

def _softmax(x, axis=-1):
    return jax.nn.softmax(x, axis=axis)

def _gelu(x):
    return jax.nn.gelu(x, approximate=True)

def _silu(x):
    return jax.nn.silu(x)

def _sigmoid(x):
    return jax.nn.sigmoid(x)

def _layernorm(x, axis=-1, eps=1e-05):
    m = jnp.mean(x, axis=axis, keepdims=True)
    v = jnp.var(x, axis=axis, keepdims=True)
    return (x - m) / jnp.sqrt(v + eps)

def _scatter_add(tgt, idx, src, axis=0):
    return tgt.at[idx].add(src)

def _segment_sum(src, seg, n):
    return jax.ops.segment_sum(src, seg, n)
kernel_name = 'mk_decoder_preln_d1_seqx_r4_ffcc0d'

def setup_inputs(seed: int=0):
    np.random.seed(seed)
    _w = jnp.asarray

    def _rec_inputs():
        import jax
        import jax.numpy as jnp
        _rk = jax.random.key(seed)
        x = 0.0001212 + 1 * jax.random.normal(jax.random.fold_in(_rk, 1), (8, 256, 1024), jnp.float32)
        _lenS = 256 - jax.random.randint(jax.random.fold_in(_rk, 7), (8,), 0, max(1, 256 // 4) + 1, jnp.int32)
        _lenS2 = 256 - jax.random.randint(jax.random.fold_in(_rk, 8), (8,), 0, max(1, 256 // 4) + 1, jnp.int32)
        _ctx_4096P = jax.random.normal(jax.random.fold_in(_rk, 11), (8, 16, 1024), jnp.float32)
        _ctx_4096c = jax.random.dirichlet(jax.random.fold_in(_rk, 511), 0.3 * jnp.ones((16,), jnp.float32), (8, 256))
        _ctx_4096t = jnp.einsum('bsk,bkd->bsd', _ctx_4096c, _ctx_4096P)
        _ctx_4096t = _ctx_4096t * jax.lax.rsqrt(jnp.mean(jnp.square(_ctx_4096t)) + 1e-12) * 0.953939
        ctx_4096 = -0.000125008 + 0.999885 * (_ctx_4096t + 0.3 * jax.random.normal(jax.random.fold_in(_rk, 611), (8, 256, 1024), jnp.float32))
        return (x, ctx_4096)
    x, ctx_4096 = _rec_inputs()

    def _L0_attn_setup():
        import jax, jax.numpy as jnp
        import numpy as np
        H = 32
        HKV = 8
        D = 1024
        HD = D // H
        S = 256
        MASK_OUT = 0.9
        MIN_REMAIN = 128
        THETA = 10000.0

        def rope_tables(seq_len, hd):
            inv_freq = 1.0 / THETA ** (jnp.arange(0, hd, 2, dtype=jnp.float32) / hd)
            t = jnp.arange(seq_len, dtype=jnp.float32)
            freqs = jnp.outer(t, inv_freq)
            emb = jnp.concatenate([freqs, freqs], axis=-1)
            return (jnp.cos(emb), jnp.sin(emb))

        def rotate_half(x):
            x1, x2 = jnp.split(x, 2, axis=-1)
            return jnp.concatenate([-x2, x1], axis=-1)

        def apply_rope(x, cos, sin):
            return x * cos + rotate_half(x) * sin
        key = jax.random.key(seed)
        k0, k1, k2, k3, k4 = jax.random.split(key, 5)
        hidden_states = jax.random.normal(k0, (1, S, D), jnp.float32)
        Wq = jax.random.normal(k1, (D, D), jnp.float32) * 0.02
        Wk = jax.random.normal(k2, (HKV * HD, D), jnp.float32) * 0.02
        Wv = jax.random.normal(k3, (HKV * HD, D), jnp.float32) * 0.02
        Wo = jax.random.normal(k4, (D, D), jnp.float32) * 0.02
        return {'hidden_states': hidden_states, 'Wq': Wq, 'Wk': Wk, 'Wv': Wv, 'Wo': Wo}
    _L0_attn_all = _L0_attn_setup()
    _L0_attn_in = {k: v for k, v in _L0_attn_all.items() if k in ('Wq', 'Wk', 'Wv', 'Wo')}
    del _L0_attn_all

    def _L0_xattn_setup():
        import jax, jax.numpy as jnp
        import numpy as np
        N, C, S = (16, 128, 1024)
        rng = jax.random.key(seed)
        k1, k2, k3 = jax.random.split(rng, 3)
        return {'key': jax.random.normal(k1, (N, C, S), dtype=jnp.float32), 'value': jax.random.normal(k2, (N, C, S), dtype=jnp.float32), 'query': jax.random.normal(k3, (N, C, S), dtype=jnp.float32)}
    _L0_xattn_all = _L0_xattn_setup()
    _L0_xattn_in = {k: v for k, v in _L0_xattn_all.items() if k in ()}
    del _L0_xattn_all

    def _L0_ffn_setup():
        import jax, jax.numpy as jnp
        import numpy as np
        IN_F = 1024
        OUT_F = 1024
        N_CLUSTERS = 64
        THRESHOLD = 0.01
        TEMPERATURE = 0.1
        BATCH, SEQ = (4, 512)
        key = jax.random.key(seed)
        k1, k2, k3, k4, k5 = jax.random.split(key, 5)
        s = 1.0 / np.sqrt(IN_F)
        return {'input': jax.random.normal(k1, (BATCH, SEQ, IN_F), dtype=jnp.float32), 'weight': jax.random.normal(k2, (OUT_F, IN_F), dtype=jnp.float32) * s, 'bias': jax.random.uniform(k3, (OUT_F,), dtype=jnp.float32, minval=-s, maxval=s), 'centroids': jax.random.normal(k4, (N_CLUSTERS, IN_F), dtype=jnp.float32) * s, 'assignments': jax.random.randint(k5, (OUT_F,), 0, N_CLUSTERS, dtype=jnp.int32)}
    _L0_ffn_all = _L0_ffn_setup()
    _L0_ffn_in = {k: v for k, v in _L0_ffn_all.items() if k in ('weight', 'bias', 'centroids', 'assignments')}
    del _L0_ffn_all
    return {'x': x, 'ctx_4096': ctx_4096, 'L0_attn_Wq': _L0_attn_in['Wq'], 'L0_attn_Wk': _L0_attn_in['Wk'], 'L0_attn_Wv': _L0_attn_in['Wv'], 'L0_attn_Wo': _L0_attn_in['Wo'], 'L0_ffn_weight': _L0_ffn_in['weight'], 'L0_ffn_bias': _L0_ffn_in['bias'], 'L0_ffn_centroids': _L0_ffn_in['centroids'], 'L0_ffn_assignments': _L0_ffn_in['assignments']}

def reference(x, ctx_4096, L0_attn_Wq, L0_attn_Wk, L0_attn_Wv, L0_attn_Wo, L0_ffn_weight, L0_ffn_bias, L0_ffn_centroids, L0_ffn_assignments):
    import jax
    import jax.numpy as jnp

    def _L0_attn_ref(hidden_states, Wq, Wk, Wv, Wo):
        import jax, jax.numpy as jnp
        import numpy as np
        H = 32
        HKV = 8
        D = 1024
        HD = D // H
        S = 256
        MASK_OUT = 0.9
        MIN_REMAIN = 128
        THETA = 10000.0

        def rope_tables(seq_len, hd):
            inv_freq = 1.0 / THETA ** (jnp.arange(0, hd, 2, dtype=jnp.float32) / hd)
            t = jnp.arange(seq_len, dtype=jnp.float32)
            freqs = jnp.outer(t, inv_freq)
            emb = jnp.concatenate([freqs, freqs], axis=-1)
            return (jnp.cos(emb), jnp.sin(emb))

        def rotate_half(x):
            x1, x2 = jnp.split(x, 2, axis=-1)
            return jnp.concatenate([-x2, x1], axis=-1)

        def apply_rope(x, cos, sin):
            return x * cos + rotate_half(x) * sin
        B, Sq, Dm = hidden_states.shape
        dtype = hidden_states.dtype
        neg = jnp.finfo(dtype).min
        q = (hidden_states @ Wq.T).reshape(B, Sq, H, HD).transpose(0, 2, 1, 3)
        k = (hidden_states @ Wk.T).reshape(B, Sq, HKV, HD).transpose(0, 2, 1, 3)
        v = (hidden_states @ Wv.T).reshape(B, Sq, HKV, HD).transpose(0, 2, 1, 3)
        rep = H // HKV
        k = jnp.repeat(k, rep, axis=1)
        v = jnp.repeat(v, rep, axis=1)
        cos, sin = rope_tables(Sq, HD)
        qr = apply_rope(q, cos, sin)
        kr = apply_rope(k, cos, sin)
        draft = jnp.einsum('bhqd,bhkd->bhqk', qr, kr)
        qi = jnp.arange(Sq)
        ki = jnp.arange(Sq)
        causal_future = qi[:, None] < ki[None, :]
        draft = draft + jnp.where(causal_future, neg, jnp.asarray(0.0, dtype))
        num_remain = max(min(Sq, MIN_REMAIN), Sq - int(Sq * MASK_OUT))
        _, draft_indices = jax.lax.top_k(draft, num_remain)
        mask = jnp.full((B, H, Sq, Sq), neg, dtype)
        b_idx = jnp.arange(B)[:, None, None, None]
        h_idx = jnp.arange(H)[None, :, None, None]
        s_idx = jnp.arange(Sq)[None, None, :, None]
        mask = mask.at[b_idx, h_idx, s_idx, draft_indices].set(0.0)
        mask = jnp.where(causal_future[None, None, :, :], neg, mask)
        scores = jnp.einsum('bhqd,bhkd->bhqk', qr, kr) / np.sqrt(HD).astype(np.float32) + mask
        attn = jax.nn.softmax(scores, axis=-1)
        out = jnp.einsum('bhqk,bhkd->bhqd', attn, v)
        out = out.transpose(0, 2, 1, 3).reshape(B, Sq, Dm)
        return out @ Wo.T

    def _L0_xattn_ref(key, value, query):
        import jax, jax.numpy as jnp
        import numpy as np
        N, C, S = (16, 128, 1024)
        KC = key.shape[1]
        sim = jnp.einsum('ncs,nds->ncd', key, query) * KC ** (-0.5)
        sim = jax.nn.softmax(sim, axis=1)
        context = jnp.einsum('ncd,nds->ncs', sim, value)
        return context

    def _L0_ffn_ref(input, weight, bias, centroids, assignments):
        import jax, jax.numpy as jnp
        import numpy as np
        IN_F = 1024
        OUT_F = 1024
        N_CLUSTERS = 64
        THRESHOLD = 0.01
        TEMPERATURE = 0.1
        BATCH, SEQ = (4, 512)
        shape = input.shape
        x = input.reshape(-1, shape[-1])
        dots = jax.nn.softmax(x @ centroids.T / TEMPERATURE, axis=-1)
        hits = dots > THRESHOLD
        query_sel = jnp.any(hits, axis=1)
        cluster_sel = jnp.any(hits, axis=0)
        row_sel = cluster_sel[assignments]
        dense = x @ weight.T + bias
        out = jnp.where(query_sel[:, None] & row_sel[None, :], dense, jnp.zeros((), dense.dtype))
        return out.reshape(*shape[:-1], -1)
    x = x + _L0_attn_ref(_layernorm(x, axis=-1), L0_attn_Wq, L0_attn_Wk, L0_attn_Wv, L0_attn_Wo)
    x = x + _L0_xattn_ref(ctx_4096, ctx_4096, _layernorm(x, axis=-1))
    x = x + _L0_ffn_ref(_layernorm(x, axis=-1), L0_ffn_weight, L0_ffn_bias, L0_ffn_centroids, L0_ffn_assignments)
    return x

_drawn_inputs = setup_inputs


def setup_inputs(seed=0):
    import zlib

    import numpy as np

    out = dict(_drawn_inputs(seed))
    spreads = {}
    factors = {'L0_ffn_bias': 5.149}
    for name, (base, spread) in spreads.items():
        noise = np.random.default_rng([zlib.crc32(name.encode()), seed]).standard_normal(out[name].shape)
        drawn = base * np.exp(spread * noise) if base else spread * noise
        out[name] = jnp.asarray(drawn.astype(out[name].dtype))
    for name, factor in factors.items():
        out[name] = (out[name] * factor).astype(out[name].dtype)
    return out
```

```python
from contextlib import ExitStack

import concourse.bass as bass
from concourse import mybir

ALU = mybir.AluOpType
ACT = mybir.ActivationFunctionType
AX = mybir.AxisListType
F32 = mybir.dt.float32
I32 = mybir.dt.int32
BF16 = mybir.dt.bfloat16

P = 128
B, S, D = 8, 256, 1024
H, HKV, HD = 32, 8, 32
REP = H // HKV
KT_ = D // P
NT = S // P
NG = HKV // 4
QG = S // 32
KEEP = 128
LO = KEEP // 32
NC = 64
SCALE = float(HD) ** -0.5
XSCALE = float(S) ** -0.5
EPS = 1e-5
NEG = -2.0 ** 100
WIN = 8
TARGET = KEEP - (WIN - 1) / 2
RING = 3
COUNTS = 4


def width(qg):
    return 32 * (qg + 1)


HOFF = [0]
for _g in range(LO, QG):
    HOFF.append(HOFF[-1] + 4 * width(_g))


def stage1_jobs():
    jobs = [("xT", t, h) for t in range(NT) for h in range(2)]
    jobs += [("q", 0), ("q", 1)]
    for n in range(4):
        jobs.append(("rot", n))
        if n < 2:
            jobs.append(("q", n + 2))
        elif n == 2:
            jobs.append(("k",))
        else:
            jobs += [("v", t) for t in range(NT)]
    jobs.append(("rot", 4))
    for G in range(NG):
        for qg in range(LO):
            jobs += [("pT", G, qg, 0), ("o", G, qg)]
        jobs.append(("flag", G))
        for qg in range(LO, QG):
            jobs += [("pT", G, qg, 0), ("pT", G, qg, 1), ("o", G, qg)]
    jobs += [("wo", t, h) for t in range(NT) for h in range(2)]
    assert len(jobs) % 2 == 0
    return jobs


def stage2_jobs():
    jobs = []
    for t in range(NT):
        jobs += [("nT", t, 0), ("nT", t, 1), ("sim", t)]
    jobs += [("ctx", c, h) for c in range(NT) for h in range(2)]
    for t in range(NT):
        jobs += [("mT", t, 0), ("mT", t, 1), ("cent", t), ("dense", t, 0), ("dense", t, 1)]
    assert len(jobs) % 2 == 0
    return jobs


def build(nc, x, ctx_kv, ctx_t, wqkv, wo, wf, cent, bias, assign, tables, masks, probe, out, x2_dram):
    with ExitStack() as st:
        def sb(name, shape, dt=F32):
            return st.enter_context(nc.sbuf_tensor(name, shape, dt))

        def sem(name):
            return st.enter_context(nc.semaphore(name))

        wqkv_sb = sb("wqkv_sb", [P, KT_, D + 2 * HKV * HD])
        wo_sb = sb("wo_sb", [P, KT_, D])
        wf_sb = sb("wf_sb", [P, KT_, D])
        cent_sb = sb("cent_sb", [P, KT_, NC])
        cos_sin = sb("cos_sin", [P, 2, S])
        mask_sb = sb("mask_sb", [P, 3 * P + 32])
        ident, rotate, spread = (mask_sb[:, j * P:(j + 1) * P] for j in range(3))
        future = mask_sb[:, 3 * P:3 * P + 32]
        row_sb = sb("row_sb", [P, 3 * 16 + 16 * WIN + 1])
        probe_sb = row_sb[:, 0:48].rearrange("p (a n) -> p a n", a=3)
        iota8 = row_sb[:, 48:48 + 16 * WIN].rearrange("p (a n) -> p a n", a=16)
        cluster_id = row_sb[:, 48 + 16 * WIN:]
        ones = sb("ones", [P, P])
        bias_sb = sb("bias_sb", [1, D])
        half = sb("half", [P, 32])
        work = sb("work", [P, NT * D])
        x_sb = work[:, :].rearrange("p (t d) -> p t d", t=NT)
        e_sb = work[:, 0:4 * S]
        pT_sb = work[:, 4 * S:8 * S].rearrange("p (k n) -> p k n", k=2)
        xn = sb("xn", [P, D])
        xT = sb("xT", [P, KT_, S])
        oT = xT
        qT = sb("qT", [P, NG, QG, REP * 32])
        kT = sb("kT", [P, NG, S])
        v_sb = sb("v_sb", [P, NT, HKV * HD])
        q_raw = sb("q_raw", [P, 2 * S])
        q_work = sb("q_work", [P, 4 * S])
        q_cos, q_sin = q_work[:, 0:2 * S], q_work[:, 2 * S:]
        below = q_work[:, 0:RING * S].rearrange("p (r s) -> p r s", r=RING)
        s_sb = sb("s_sb", [P, HOFF[-1]])
        hit = sb("hit", [P, RING, S], BF16)
        act_junk = sb("act_junk", [P, RING, S], BF16)
        o_scale = sb("o_scale", [P, P])
        ssum = sb("ssum", [P, 2, 16])
        nmax = sb("nmax", [P, QG, 4])
        bmax = sb("bmax", [P, QG, 4])
        tq = sb("tq", [P, 2, 16])
        dq = sb("dq", [P, 2, 16])
        sd = sb("sd", [P, 16])
        step = sb("step", [P, 3, 16])
        tmp = sb("tmp", [P, 4, 16])
        cand = sb("cand", [P, 16, WIN + 1])
        pick = sb("pick", [P, 16, WIN])
        prod = sb("prod", [P, 16, WIN])
        thr = sb("thr", [P, 2, 16])
        fail = sb("fail", [P, 16])
        flag_f = sb("flag_f", [1, 17])
        flag_i = sb("flag_i", [1, 17], I32)
        top8 = sb("top8", [P, 8])
        stats = sb("stats", [P, 12])
        mv = sb("mv", [P, 2])
        rstd = sb("rstd", [P, 1])
        veps = sb("veps", [P, 1])
        x1 = sb("x1", [P, NT, D])
        nT = sb("nT", [P, KT_, P])
        ctx_sb = sb("ctx_sb", [P, NT * D])
        ctxT_sb = ctx_sb[:, :].rearrange("p (k s) -> p k s", k=KT_)
        ctxv_sb = ctx_sb[:, :].rearrange("p (t d) -> p t d", t=NT)
        p2 = sb("p2", [P, NT, S])
        small = sb("small", [P, 4])
        gate = sb("gate", [P, 2, NC])
        hits = sb("hits", [P, NC])
        o_sb = sb("o_sb", [P, D])

        assign_sb = xT[0:NC, 0:4, :].rearrange("p k n -> p (k n)").bitcast(I32)
        one_hot = s_sb[0:NC, 0:D]
        row_on = wo_sb[:, 0, :].rearrange("p (h n) -> p h n", h=2)
        row_off = wo_sb[:, 1, :].rearrange("p (h n) -> p h n", h=2)
        fix_a, fix_b = wo_sb[:, 2, :], wo_sb[:, 3, :]

        quad = st.enter_context(nc.psum_tensor("quad", [P, 4, 512], F32))
        acc1 = [st.enter_context(nc.psum_tensor(f"acc1_{j}", [P, 512], F32)) for j in range(2)]
        acc2 = [st.enter_context(nc.psum_tensor(f"acc2_{j}", [P, 512], F32)) for j in range(2)]

        tables_in, wqkv_in, wo_in, wf_in, consts_ready = map(sem, ("tables_in", "wqkv_in", "wo_in", "wf_in", "consts_ready"))
        x_in, xres_in, ctxT_in, ctxv_in = map(sem, ("x_in", "xres_in", "ctxT_in", "ctxv_in"))
        full1 = [sem(f"full1_{j}") for j in range(2)]
        free1 = [sem(f"free1_{j}") for j in range(2)]
        full2 = [sem(f"full2_{j}") for j in range(2)]
        free2 = [sem(f"free2_{j}") for j in range(2)]
        var1, rstd1, xn1 = sem("var1"), sem("rstd1"), sem("xn1")
        var2, rstd2, xn2 = sem("var2"), sem("rstd2"), sem("xn2")
        q_cos_ready, qk_ready = sem("q_cos_ready"), sem("qk_ready")
        s_full, s_free, s_stats = sem("s_full"), sem("s_free"), sem("s_stats")
        var_s, sd_ready = sem("var_s"), sem("sd_ready")
        bmax_ready, e_ready, p_ready, fail_ready, exact_done = map(
            sem, ("bmax_ready", "e_ready", "p_ready", "fail_ready", "exact_done"))
        x2_out, o_out, smax_ready, p2_ready, gmax_ready = map(
            sem, ("x2_out", "o_out", "smax_ready", "p2_ready", "gmax_ready"))
        dve1, dve2, ln_step = sem("dve_step1"), sem("dve_step2"), sem("ln_step")
        passed = sem("passed")
        fin_sel, fin_pe, fin_step, rows_ready, fix_in, fix_step, fix_out, cluster_ready, assign_in = map(
            sem, ("fin_sel", "fin_pe", "fin_step", "rows_ready", "fix_in", "fix_step", "fix_out", "cluster_ready", "assign_in"))

        J1, J2 = stage1_jobs(), stage2_jobs()
        at1 = {j: (n % 2, n // 2) for n, j in enumerate(J1)}
        at2 = {j: (n % 2, n // 2) for n, j in enumerate(J2)}
        N1, N2 = len(J1) // 2, len(J2) // 2

        def wait(eng, s, b, per, k):
            v = b * per + k
            if isinstance(v, int) and v <= 0:
                return
            eng.wait_ge(s, v)

        def settle(eng):
            eng.sem_inc(passed, 1)

        class Bank:
            def __init__(self, stage, job):
                banks, full, free, at, self.per = ((acc1, full1, free1, at1, N1), (acc2, full2, free2, at2, N2))[stage - 1]
                j, self.n = at[job]
                self.ps, self.full, self.free = banks[j], full[j], free[j]

            def wait_free(self, eng, b):
                wait(eng, self.free, b, self.per, self.n)

            def wait_read(self, eng, b):
                wait(eng, self.free, b, self.per, self.n + 1)

            def wait_full(self, eng, b):
                wait(eng, self.full, b, self.per, self.n + 1)

        def sgroup(G, qg):
            return 8 * G + (qg - LO if qg >= LO else qg + QG - LO)

        def s_tiles(qg):
            o = HOFF[qg - LO]
            return s_sb[:, o:o + 4 * width(qg)].rearrange("p (i w) -> p i w", i=4)

        def last_part(G, qg):
            return ("pT", G, qg, 1 if qg >= LO else 0)

        block = st.enter_context(nc.Block())

        @block.sync
        def _(sp):
            sp.dma_start(cos_sin[:, :, :], tables).then_inc(tables_in, 16)
            sp.dma_start(mask_sb[:, :], masks).then_inc(tables_in, 16)
            sp.dma_start(row_sb[:, :], probe).then_inc(tables_in, 16)
            sp.dma_start(bias_sb[:, :], bias).then_inc(tables_in, 16)

            def load_x(b):
                if not (isinstance(b, int) and b == 0):
                    Bank(1, ("o", NG - 1, QG - 1)).wait_full(sp, b - 1)
                sp.dma_start(x_sb, x[b].rearrange("(t p) d -> p t d", p=P)).then_inc(x_in, 16)

            def load_res(b):
                wait(sp, x2_out, b, 32, 0)
                if not (isinstance(b, int) and b == 0):
                    Bank(2, ("dense", NT - 1, 1)).wait_read(sp, b - 1)
                sp.dma_start(x1[:, :, :], x[b].rearrange("(t p) d -> p t d", p=P)).then_inc(xres_in, 16)

            def load_ctx_values(b):
                Bank(2, ("sim", NT - 1)).wait_full(sp, b)
                sp.dma_start(ctxv_sb, ctx_kv[b].rearrange("(t p) d -> p t d", p=P)).then_inc(ctxv_in, 16)

            def load_ctx(b):
                if not (isinstance(b, int) and b == 0):
                    Bank(2, ("ctx", NT - 1, 1)).wait_full(sp, b - 1)
                sp.dma_start(ctxT_sb, ctx_t[b].rearrange("(k p) s -> p k s", p=P)).then_inc(ctxT_in, 16)

            def store(b):
                for t in range(NT):
                    Bank(2, ("ctx", t, 1)).wait_read(sp, b)
                    sp.dma_start(x2_dram[b, t * P:(t + 1) * P, :], x1[:, t, :]).then_inc(x2_out, 16)
                for t in range(NT):
                    Bank(2, ("dense", t, 1)).wait_read(sp, b)
                    sp.dma_start(out[b, t * P:(t + 1) * P, :], o_sb[:, :]).then_inc(o_out, 16)

            load_x(0)
            sp.dma_start(wqkv_sb[:, :, :], wqkv.rearrange("(k p) n -> p k n", p=P)).then_inc(wqkv_in, 16)
            load_ctx(0)
            load_res(0)
            sp.dma_start(wo_sb[:, :, :], wo.rearrange("(k p) n -> p k n", p=P)).then_inc(wo_in, 16)
            sp.dma_start(cent_sb[:, :, :], cent.rearrange("(k p) n -> p k n", p=P)).then_inc(wf_in, 16)
            sp.dma_start(wf_sb[:, :, :], wf.rearrange("(k p) n -> p k n", p=P)).then_inc(wf_in, 16)
            with sp.Fori(1, B) as b:
                load_x(b)
                load_ctx_values(b - 1)
                store(b - 1)
                load_ctx(b)
                load_res(b)
            Bank(1, ("wo", NT - 1, 1)).wait_full(sp, B - 1)
            sp.dma_start(assign_sb, assign).then_inc(assign_in, 16)
            load_ctx_values(B - 1)
            store(B - 1)
            sp.wait_ge(x2_out, 32 * B)
            sp.wait_ge(o_out, 16 * NT * B)

        @block.tensor
        def _(pe):
            def begin(stage, job, b):
                bank = Bank(stage, job)
                bank.wait_free(pe, b)
                return bank

            def transposes(stage, job, b, src, n=4):
                bank = begin(stage, job, b)
                for j in range(n):
                    mm = pe.transpose(bank.ps[:, j * P:(j + 1) * P], src(j), ident)
                mm.then_inc(bank.full, 1)
                return mm

            def product(bank, dst, lhs, rhs, steps=KT_):
                for k in range(steps):
                    mm = pe.matmul(dst, lhs(k), rhs(k), start=(k == 0), stop=(k == steps - 1))
                return mm

            def normed_T(b):
                for t in range(NT):
                    wait(pe, xn1, b, NT, t + 1)
                    for h in range(2):
                        transposes(1, ("xT", t, h), b, lambda j: xn[:, (4 * h + j) * P:(4 * h + j + 1) * P])

            def qkv(b):
                def q_pair(n, job):
                    bank = begin(1, job, b)
                    for a in range(2):
                        m = 2 * n + a
                        mm = product(bank, bank.ps[:, a * S:(a + 1) * S],
                                     lambda k: wqkv_sb[:, k, m * P:(m + 1) * P], lambda k: xT[:, k, :])
                    mm.then_inc(bank.full, 1)

                def rot(n):
                    Bank(1, ("q", n) if n < 4 else ("k",)).wait_read(pe, b)
                    bank = begin(1, ("rot", n), b)
                    pe.matmul(bank.ps[:, :], rotate, q_raw[:, :], start=True, stop=True).then_inc(bank.full, 1)

                Bank(1, ("xT", NT - 1, 1)).wait_read(pe, b)
                q_pair(0, ("q", 0))
                q_pair(1, ("q", 1))
                for n in range(4):
                    rot(n)
                    if n < 2:
                        q_pair(n + 2, ("q", n + 2))
                    elif n == 2:
                        q_pair(4, ("k",))
                    else:
                        for t in range(NT):
                            bank = begin(1, ("v", t), b)
                            product(bank, bank.ps[:, 0:HKV * HD], lambda k: xT[:, k, t * P:(t + 1) * P],
                                    lambda k: wqkv_sb[:, k, D + HKV * HD:]).then_inc(bank.full, 1)
                rot(4)

            def scores(b, G, qg):
                if sgroup(G, qg) == 0:
                    wait(pe, qk_ready, b, 5, 5)
                wait(pe, s_free, b, 16, sgroup(G, qg))
                w = width(qg)
                for i in range(4):
                    r = slice(32 * i, 32 * i + 32)
                    pe.matmul(quad[:, i, 0:w], qT[r, G, qg, :], kT[r, G, 0:w],
                              start=True, stop=False, skip_group_check=True)
                for i in range(4):
                    r = slice(32 * i, 32 * i + 32)
                    mm = pe.matmul(quad[:, i, w - 32:w], spread[r, :], future[r, :],
                                   start=False, stop=True, skip_group_check=True)
                mm.then_inc(s_full, 1)

            def attend(b, G, qg):
                w = width(qg)
                if qg < LO:
                    wait(pe, s_free, b, 16, sgroup(G, qg) + 1)
                else:
                    wait(pe, p_ready, b, 8, 4 * G + qg - LO + 1)
                parts = [(0, min(w, P))] + ([(1, w - P)] if w > P else [])
                for kb, rows in parts:
                    bank = begin(1, ("pT", G, qg, kb), b)
                    settle(pe)
                    for i in range(4):
                        o = i * w + kb * P
                        mm = pe.transpose(bank.ps[0:rows, i * P:(i + 1) * P], e_sb[:, o:o + rows], ident)
                    mm.then_inc(bank.full, 1)
                bank = begin(1, ("o", G, qg), b)
                Bank(1, ("pT", G, qg, len(parts) - 1)).wait_read(pe, b)
                settle(pe)
                for i in range(4):
                    c = slice(32 * i, 32 * i + 32)
                    kv = 4 * G + i
                    for what in range(2):
                        for kb, rows in parts:
                            lhs = v_sb[0:rows, kb, kv * HD:(kv + 1) * HD] if what == 0 else ones[0:rows, 0:HD]
                            mm = pe.matmul(bank.ps[c, what * P:(what + 1) * P], lhs, pT_sb[0:rows, kb, i * P:(i + 1) * P],
                                           start=(what == 0 and kb == 0), stop=(kb == len(parts) - 1),
                                           skip_group_check=True)
                mm.then_inc(bank.full, 1)

            def project(b):
                Bank(1, ("o", NG - 1, QG - 1)).wait_read(pe, b)
                for t in range(NT):
                    for h in range(2):
                        bank = begin(1, ("wo", t, h), b)
                        product(bank, bank.ps[:, :], lambda k: oT[:, k, t * P:(t + 1) * P],
                                lambda k: wo_sb[:, k, h * 512:(h + 1) * 512]).then_inc(bank.full, 1)

            def norm_T(b, name, t, n):
                wait(pe, xn2, b, 2 * NT, n + 1)
                for h in range(2):
                    transposes(2, (name, t, h), b, lambda j: xn[:, (4 * h + j) * P:(4 * h + j + 1) * P])
                Bank(2, (name, t, 1)).wait_read(pe, b)

            def sim(b, t):
                norm_T(b, "nT", t, t)
                if t == 0:
                    wait(pe, ctxT_in, b, 16, 16)
                bank = begin(2, ("sim", t), b)
                product(bank, bank.ps[:, 0:S], lambda k: nT[:, k, :], lambda k: ctxT_sb[:, k, :]).then_inc(bank.full, 1)

            def context(b, c):
                if c == 0:
                    wait(pe, p2_ready, b, NT, NT)
                    wait(pe, ctxv_in, b, 16, 16)
                for h in range(2):
                    bank = begin(2, ("ctx", c, h), b)
                    product(bank, bank.ps[:, :], lambda k: p2[:, k, c * P:(c + 1) * P],
                            lambda k: ctxv_sb[:, k, h * 512:(h + 1) * 512], NT).then_inc(bank.full, 1)

            def centroids(b, t):
                norm_T(b, "mT", t, NT + t)
                bank = begin(2, ("cent", t), b)
                product(bank, bank.ps[:, 0:NC], lambda k: nT[:, k, :], lambda k: cent_sb[:, k, :]).then_inc(bank.full, 1)

            def dense(b, t):
                for h in range(2):
                    bank = begin(2, ("dense", t, h), b)
                    product(bank, bank.ps[:, :], lambda k: nT[:, k, :] if k < KT_ else ones[0:1, :],
                            lambda k: wf_sb[:, k, h * 512:(h + 1) * 512] if k < KT_ else bias_sb[0:1, h * 512:(h + 1) * 512],
                            KT_ + 1).then_inc(bank.full, 1)

            def stage2(b, G, k):
                if b is None:
                    return
                ([lambda: sim(b, 0), lambda: sim(b, 1), lambda: context(b, 0), lambda: context(b, 1)],
                 [lambda: centroids(b, 0), lambda: dense(b, 0), lambda: centroids(b, 1), lambda: dense(b, 1)])[G][k]()

            def body(b, b2):
                normed_T(b)
                qkv(b)
                for G in range(NG):
                    for qg in range(LO, QG):
                        scores(b, G, qg)
                    for k in range(LO):
                        scores(b, G, k)
                        stage2(b2, G, k)
                        attend(b, G, k)
                    bank = begin(1, ("flag", G), b)
                    wait(pe, fail_ready, b, NG, G + 1)
                    pe.matmul(bank.ps[0:1, 0:16], ones[:, 0:1], fail[:, :], start=True, stop=True).then_inc(bank.full, 1)
                    for qg in range(LO, QG):
                        attend(b, G, qg)
                project(b)

            pe.wait_ge(tables_in, 64)
            pe.wait_ge(consts_ready, 1)
            pe.wait_ge(wqkv_in, 16)
            pe.wait_ge(wo_in, 16)
            pe.wait_ge(wf_in, 32)
            body(0, None)
            with pe.Fori(1, B) as b:
                body(b, b - 1)
            for G in range(NG):
                for k in range(4):
                    stage2(B - 1, G, k)
            pe.wait_ge(fin_sel, 1)
            pe.matmul(quad[0:NC, 0, 0:1], hits[:, :], ones[:, 0:1], start=True, stop=True).then_inc(fin_pe, 1)
            pe.wait_ge(cluster_ready, 1)
            for h in range(2):
                mm = pe.matmul(quad[:, h + 1, :], e_sb[0:NC, 0:P], one_hot[:, h * 512:(h + 1) * 512], start=True, stop=True)
            mm.then_inc(fin_pe, 1)

        @block.vector
        def _(dve):
            v = nc.vector

            class Chain:
                def __init__(self, s, per):
                    self.s, self.per, self.b, self.k = s, per, 0, 0

                def start(self, b):
                    self.b, self.k = b, 0

                def put(self, ins):
                    self.k += 1
                    ins.then_inc(self.s, 1)
                    return self.k

                def upto(self, k, apart=False):
                    wait(dve, self.s, self.b, self.per, k)
                    if apart:
                        settle(dve)

                def __call__(self, ins, apart=False):
                    self.k += 1
                    ins.then_inc(self.s, 1)
                    wait(dve, self.s, self.b, self.per, self.k)
                    if apart:
                        settle(dve)

            c1, c2 = Chain(dve1, CHAIN1), Chain(dve2, CHAIN2)

            v.memset(ones[:, :], 1.0)
            v.memset(hits[:, :], 0.0)
            v.memset(half[:, 0:16], 0.5)
            v.memset(half[:, 16:32], -0.5).then_inc(consts_ready, 1)
            dve.wait_ge(consts_ready, 1)
            dve.wait_ge(tables_in, 64)

            def layer_norm(b, n, per, src, link, var_sem, rstd_sem, xn_sem, xn_free):
                for h in range(2):
                    ins = v.bn_stats(stats[:, 6 * h:6 * h + 6], src[:, h * 512:(h + 1) * 512])
                link(ins, apart=True)
                link(v.bn_aggr(mv[:, :], stats[:, :]))
                v.tensor_scalar(veps[:, :], mv[:, 1:2], EPS, None, ALU.add).then_inc(var_sem, 1)
                xn_free()
                wait(dve, rstd_sem, b, per, n + 1)
                v.tensor_scalar(xn[:, :], src, mv[:, 0:1], rstd[:, 0:1], ALU.subtract, ALU.mult).then_inc(xn_sem, 1)

            def ln1(b, t):
                def xn_free():
                    if t:
                        Bank(1, ("xT", t - 1, 1)).wait_full(dve, b)
                if t == 0:
                    wait(dve, x_in, b, 16, 16)
                layer_norm(b, t, NT, x_sb[:, t, :], c1, var1, rstd1, xn1, xn_free)

            def ln2(b, n, last=False):
                t = n % NT

                def xn_free():
                    if n == 0 and not last:
                        Bank(1, ("xT", NT - 1, 1)).wait_full(dve, b + 1)
                    elif n > 0:
                        Bank(2, ("nT" if n <= NT else "mT", (n - 1) % NT, 1)).wait_full(dve, b)
                layer_norm(b, n, 2 * NT, x1[:, t, :], c2, var2, rstd2, xn2, xn_free)

            def rope(b):
                for n in range(5):
                    bank = Bank(1, ("rot", n))
                    bank.wait_full(dve, b)
                    wait(dve, qk_ready, b, 5, n)
                    v.tensor_tensor(q_sin[:, :].rearrange("p (a s) -> p a s", a=2), bank.ps[:, :].rearrange("p (a s) -> p a s", a=2),
                                    cos_sin[:, 1:2, :].to_broadcast([P, 2, S]), ALU.mult).then_inc(bank.free, 1)

            def tile(n):
                return s_tiles(LO + n // 4)[:, n % 4, :]

            def upper_setup(b, G):
                for qg in range(LO, QG):
                    wait(dve, s_free, b, 16, sgroup(G, qg) + 1)
                    ins = v.tensor_reduce(nmax[:, qg, :], s_tiles(qg), AX.X, ALU.max, negate=True)
                c1(ins)
                v.tensor_scalar(bmax[:, LO:, :], nmax[:, LO:, :], SCALE, None, ALU.mult).then_inc(bmax_ready, 1)
                wait(dve, s_stats, b, 32 * NG, 32 * G + 32)
                mu, ex2 = ssum[:, 0, :], ssum[:, 1, :]
                v.tensor_tensor(tmp[:, 0, :], mu, probe_sb[:, 2, :], ALU.mult)
                c1(v.tensor_tensor(tmp[:, 1, :], ex2, probe_sb[:, 2, :], ALU.mult))
                c1(v.tensor_tensor(tmp[:, 2, :], tmp[:, 0, :], tmp[:, 0, :], ALU.mult))
                c1(v.tensor_tensor(tmp[:, 1, :], tmp[:, 1, :], tmp[:, 2, :], ALU.subtract))
                v.tensor_scalar(tmp[:, 1, :], tmp[:, 1, :], 1e-30, None, ALU.max).then_inc(var_s, 1)
                wait(dve, sd_ready, b, NG, G + 1)
                c1(v.tensor_tensor(tmp[:, 2, :], sd[:, :], probe_sb[:, 0, :], ALU.mult))
                v.tensor_tensor(tq[:, 0, :], tmp[:, 0, :], tmp[:, 2, :], ALU.add)
                c1(v.tensor_tensor(step[:, 0, :], sd[:, :], probe_sb[:, 1, :], ALU.mult))
                v.tensor_scalar(step[:, 1, :], step[:, 0, :], 0.3, None, ALU.mult)
                c1(v.tensor_scalar(step[:, 2, :], step[:, 0, :], 3.0, None, ALU.mult))

            def count(k):
                new = k % 2
                counted, lowered, listed = [], [], []

                def count_tile(n):
                    w = width(LO + n // 4)
                    if n >= RING:
                        c1.upto((lowered if k == COUNTS - 1 else counted)[n - RING])
                    counted.append(c1.put(v.tensor_scalar(hit[:, n % RING, 0:w], tile(n), tq[:, new, n:n + 1], -TARGET,
                                                          ALU.is_ge, ALU.add, accum_out=dq[:, new, n:n + 1])))

                def lower_tile(n):
                    w = width(LO + n // 4)
                    c1.upto(max(counted[n], listed[n - RING] if n >= RING else 0))
                    lowered.append(c1.put(v.scalar_tensor_tensor(below[:, n % RING, 0:w], hit[:, n % RING, 0:w], NEG, tile(n),
                                                                 ALU.mult, ALU.add)))

                def list_tile(n):
                    w = width(LO + n // 4)
                    c1.upto(lowered[n], apart=True)
                    listed.append(c1.put(v.max(cand[:, n, 1:WIN + 1], below[:, n % RING, 0:w])))

                for n in range(16 + (2 if k == COUNTS - 1 else 0)):
                    if n < 16:
                        count_tile(n)
                    if k == COUNTS - 1:
                        if 1 <= n <= 16:
                            lower_tile(n - 1)
                        if n >= 2:
                            list_tile(n - 2)
                c1.upto(c1.k)

            def update(k):
                new, old = k % 2, (k + 1) % 2
                t, d = tq[:, new, :], dq[:, new, :]
                slope = step[:, 0, :]
                if k:
                    slope = tmp[:, 0, :]
                    v.tensor_tensor(tmp[:, 1, :], dq[:, old, :], d, ALU.subtract)
                    c1(v.tensor_tensor(tmp[:, 0, :], t, tq[:, old, :], ALU.subtract))
                    v.tensor_tensor(tmp[:, 0, :], tmp[:, 0, :], tmp[:, 1, :], ALU.mult)
                    c1(v.tensor_tensor(tmp[:, 2, :], tmp[:, 1, :], tmp[:, 1, :], ALU.mult))
                    c1(v.tensor_scalar(tmp[:, 2, :], tmp[:, 2, :], 1.0, None, ALU.max))
                    c1(v.reciprocal(tmp[:, 1, :], tmp[:, 2, :]))
                    c1(v.tensor_tensor(tmp[:, 2, :], tmp[:, 0, :], tmp[:, 1, :], ALU.mult))
                    c1(v.tensor_tensor(tmp[:, 1, :], tmp[:, 2, :], step[:, 1, :], ALU.max))
                    v.tensor_tensor(tmp[:, 0, :], tmp[:, 1, :], step[:, 2, :], ALU.min)
                c1(v.tensor_tensor(tmp[:, 3, :], d, d, ALU.mult))
                c1(v.scalar_tensor_tensor(tmp[:, 3, :], tmp[:, 3, :], 13.0, d, ALU.is_gt, ALU.mult))
                c1(v.tensor_tensor(tmp[:, 3, :], tmp[:, 3, :], slope, ALU.mult))
                c1(v.tensor_tensor(tq[:, old, :], t, tmp[:, 3, :], ALU.add))

            def select(b, G):
                last = (COUNTS - 1) % 2
                v.tensor_copy(cand[:, :, 0:1], tq[:, last, :].rearrange("p (n o) -> p n o", o=1))
                c1(v.tensor_scalar(tmp[:, 0, :], dq[:, last, :], -1.0, (WIN - 1) / 2, ALU.mult, ALU.add))
                c1(v.tensor_tensor(pick[:, :, :], iota8[:, :, :],
                                   tmp[:, 0, :].rearrange("p (n o) -> p n o", o=1).to_broadcast([P, 16, WIN]), ALU.is_equal))
                for m in range(2):
                    c1(v.tensor_tensor(prod[:, :, :], pick[:, :, :], cand[:, :, m:m + WIN], ALU.mult))
                    c1(v.tensor_reduce(thr[:, m, :], prod[:, :, :], AX.X, ALU.add))
                v.tensor_tensor(fail[:, :], thr[:, 0, :], thr[:, 1, :], ALU.is_equal).then_inc(fail_ready, 1)

            def exact(b, G):
                bank = Bank(1, ("flag", G))
                bank.wait_full(dve, b)
                v.tensor_copy(flag_f[:, 0:16], bank.ps[0:1, 0:16]).then_inc(bank.free, 1)
                wait(dve, bank.free, b, bank.per, bank.n + 1)
                c1(v.tensor_reduce(flag_f[:, 16:17], flag_f[:, 0:16], AX.X, ALU.add))
                c1(v.tensor_copy(flag_i[:, :], flag_f[:, :]), apart=True)
                anywhere = dve.value_load(flag_i[0:1, 16:17])
                with dve.If(anywhere > 0):
                    for n in range(16):
                        w = width(LO + n // 4)
                        here = dve.value_load(flag_i[0:1, n:n + 1])
                        with dve.If(here > 0):
                            left, drop = below[:, 0, 0:w], below[:, 1, 0:w]
                            v.tensor_copy(left, tile(n))
                            dve.drain()
                            with dve.Fori(0, KEEP // 8) as _r:
                                v.max(top8[:, :], left)
                                dve.drain()
                                v.match_replace(left, top8[:, :], left, 2 * NEG)
                                dve.drain()
                            v.tensor_scalar(drop, left, 1.5 * NEG, NEG, ALU.is_gt, ALU.mult)
                            dve.drain()
                            v.tensor_tensor(tile(n), tile(n), drop, ALU.add)
                            v.memset(thr[:, 0, n:n + 1], 0.5 * NEG)
                            dve.drain()

            def masked(b, G, qg):
                w = width(qg)
                wait(dve, e_ready, b, 8, 4 * G + qg - LO + 1)
                for i in range(4):
                    n = 4 * (qg - LO) + i
                    ins = v.scalar_tensor_tensor(e_sb[:, i * w:(i + 1) * w], tile(n), thr[:, 0, n:n + 1],
                                                 e_sb[:, i * w:(i + 1) * w], ALU.is_ge, ALU.mult)
                ins.then_inc(p_ready, 1)

            def head_out(b, G, qg):
                bank = Bank(1, ("o", G, qg))
                bank.wait_full(dve, b)
                c1(v.reciprocal(o_scale[:, :], bank.ps[:, P:2 * P]))
                v.tensor_tensor(oT[:, 4 * G:4 * G + 4, 32 * qg:32 * qg + 32],
                                bank.ps[:, 0:P].rearrange("p (r q) -> p r q", r=REP),
                                o_scale[:, :].rearrange("p (r q) -> p r q", r=REP), ALU.mult).then_inc(bank.free, 1)

            def lower_max(b, G, qg):
                wait(dve, s_full, b, 16, sgroup(G, qg) + 1)
                c1(v.tensor_reduce(nmax[:, qg, :], quad[:, :, 0:width(qg)], AX.X, ALU.max, negate=True))
                v.tensor_scalar(bmax[:, qg, :], nmax[:, qg, :], SCALE, None, ALU.mult).then_inc(bmax_ready, 1)

            def residual(b):
                wait(dve, xres_in, b, 16, 16)
                for t in range(NT):
                    for h in range(2):
                        bank = Bank(1, ("wo", t, h))
                        bank.wait_full(dve, b)
                        xs = x1[:, t, h * 512:(h + 1) * 512]
                        v.tensor_tensor(xs, bank.ps[:, :], xs, ALU.add).then_inc(bank.free, 1)
                bank.wait_read(dve, b)

            def sim_max(b, t):
                bank = Bank(2, ("sim", t))
                bank.wait_full(dve, b)
                c2(v.tensor_reduce(small[:, 0:1], bank.ps[:, 0:S], AX.X, ALU.max, negate=True))
                v.tensor_scalar(small[:, 1:2], small[:, 0:1], XSCALE, None, ALU.mult).then_inc(smax_ready, 1)

            def sim_norm(b, t):
                Bank(2, ("sim", t)).wait_read(dve, b)
                c2(v.reciprocal(small[:, 3:4], small[:, 2:3]))
                v.tensor_scalar(p2[:, t, :], p2[:, t, :], small[:, 3:4], None, ALU.mult).then_inc(p2_ready, 1)

            def add_context(b, c):
                for h in range(2):
                    bank = Bank(2, ("ctx", c, h))
                    bank.wait_full(dve, b)
                    xs = x1[:, c, h * 512:(h + 1) * 512]
                    v.tensor_tensor(xs, bank.ps[:, :], xs, ALU.add).then_inc(bank.free, 1)
                bank.wait_read(dve, b)

            def cluster_max(b, t):
                bank = Bank(2, ("cent", t))
                bank.wait_full(dve, b)
                c2(v.tensor_reduce(small[:, 0:1], bank.ps[:, 0:NC], AX.X, ALU.max, negate=True))
                v.tensor_scalar(small[:, 1:2], small[:, 0:1], 10.0, None, ALU.mult).then_inc(gmax_ready, 1)

            def cluster_hits(b, t):
                Bank(2, ("cent", t)).wait_read(dve, b)
                c2(v.reciprocal(small[:, 3:4], small[:, 2:3]))
                c2(v.tensor_scalar(gate[:, 1, :], gate[:, 0, :], small[:, 3:4], 0.01, ALU.mult, ALU.is_gt))
                v.tensor_tensor(hits[:, :], hits[:, :], gate[:, 1, :], ALU.max)
                c2(v.tensor_reduce(small[:, 0:1], gate[:, 1, :], AX.X, ALU.max))

            def dense_out(b, t):
                n = NT * b + t
                if not (isinstance(n, int) and n == 0):
                    dve.wait_ge(o_out, 16 * n)
                for h in range(2):
                    bank = Bank(2, ("dense", t, h))
                    bank.wait_full(dve, b)
                    v.scalar_tensor_tensor(o_sb[:, h * 512:(h + 1) * 512], bank.ps[:, :], small[:, 0:1],
                                           x1[:, t, h * 512:(h + 1) * 512], ALU.mult, ALU.add).then_inc(bank.free, 1)

            def stage2(b, G, k, last=False):
                if b is None:
                    return
                if G == 0:
                    if k == 0:
                        c2.start(b)
                        sim_max(b, 0)
                        ln2(b, 1, last)
                        sim_norm(b, 0)
                    elif k == 1:
                        sim_max(b, 1)
                        sim_norm(b, 1)
                    else:
                        add_context(b, k - 2)
                        if k == 3:
                            ln2(b, 2, last)
                elif k == 0:
                    cluster_max(b, 0)
                    ln2(b, 3, last)
                    cluster_hits(b, 0)
                elif k == 2:
                    cluster_max(b, 1)
                    cluster_hits(b, 1)
                else:
                    dense_out(b, k // 2)

            def body(b, b2):
                c1.start(b)
                for t in range(NT):
                    ln1(b, t)
                if b2 is not None:
                    c2_start(b2)
                rope(b)
                for G in range(NG):
                    upper_setup(b, G)
                    for k in range(4):
                        lower_max(b, G, k)
                        count(k)
                        if k < COUNTS - 1:
                            update(k)
                        stage2(b2, G, k)
                        head_out(b, G, k)
                    select(b, G)
                    exact(b, G)
                    dve.sem_inc(exact_done, 1)
                    for qg in range(LO, QG):
                        masked(b, G, qg)
                        if qg > LO:
                            head_out(b, G, qg - 1)
                    head_out(b, G, QG - 1)
                residual(b)
                assert c1.k == CHAIN1, c1.k

            def c2_start(b, last=False):
                ln2_chain.start(b)
                layer_norm_first(b, last)

            ln2_chain = Chain(ln_step, 2)

            def layer_norm_first(b, last):
                def xn_free():
                    if not last:
                        Bank(1, ("xT", NT - 1, 1)).wait_full(dve, b + 1)
                layer_norm(b, 0, 2 * NT, x1[:, 0, :], ln2_chain, var2, rstd2, xn2, xn_free)

            body(0, None)
            with dve.Fori(1, B) as b:
                body(b, b - 1)
            assert c2.k == CHAIN2, c2.k
            c2_start(B - 1, True)
            for G in range(NG):
                for k in range(4):
                    stage2(B - 1, G, k, True)
            dve.wait_ge(assign_in, 16)
            v.tensor_scalar(one_hot, assign_sb, cluster_id[0:NC, :], None, ALU.is_equal).then_inc(fin_sel, 1)
            dve.wait_ge(fin_pe, 1)
            v.tensor_scalar(small[0:NC, 0:1], quad[0:NC, 0, 0:1], 0.0, None, ALU.is_gt).then_inc(fin_step, 1)
            dve.wait_ge(fin_step, 1)
            v.tensor_scalar(e_sb[0:NC, 0:P], ones[0:NC, :], small[0:NC, 0:1], None, ALU.mult).then_inc(cluster_ready, 1)
            dve.wait_ge(fin_pe, 2)
            v.tensor_copy(row_on, quad[:, 1:3, :])
            v.tensor_scalar(row_off, quad[:, 1:3, :], -1.0, 1.0, ALU.mult, ALU.add).then_inc(fin_step, 1)
            dve.wait_ge(fin_step, 2)
            v.tensor_reduce(flag_f[:, 0:1], row_off[0:1, :, :], AX.XY, ALU.add).then_inc(fin_step, 1)
            dve.wait_ge(fin_step, 3)
            v.tensor_copy(flag_i[:, 0:1], flag_f[:, 0:1]).then_inc(rows_ready, 1)

        @block.scalar
        def _(act):
            s = nc.scalar

            def copy_out(stage, job, b, dst, rows=P, cols=512):
                bank = Bank(stage, job)
                bank.wait_full(act, b)
                s.activation(dst, bank.ps[0:rows, 0:cols], ACT.Copy).then_inc(bank.free, 1)

            def normed_T(b):
                if not (isinstance(b, int) and b == 0):
                    Bank(1, ("wo", NT - 1, 1)).wait_full(act, b - 1)
                for t in range(NT):
                    for h in range(2):
                        bank = Bank(1, ("xT", t, h))
                        bank.wait_full(act, b)
                        s.activation(xT[:, 4 * h:4 * h + 4, t * P:(t + 1) * P],
                                     bank.ps[:, :].rearrange("p (k n) -> p k n", k=4), ACT.Copy).then_inc(bank.free, 1)

            def qkv(b):
                def raw(n, job):
                    if n:
                        Bank(1, ("rot", n - 1)).wait_full(act, b)
                        wait(act, q_cos_ready, b, 5, n)
                    copy_out(1, job, b, q_raw[:, :])

                raw(0, ("q", 0))
                raw(1, ("q", 1))
                raw(2, ("q", 2))
                raw(3, ("q", 3))
                raw(4, ("k",))
                for t in range(NT):
                    copy_out(1, ("v", t), b, v_sb[:, t, :], cols=HKV * HD)

            def upper_store(b, G):
                for qg in range(LO, QG):
                    wait(act, p_ready, b, 8, 4 * (G - 1) + qg - LO + 1)
                    wait(act, s_full, b, 16, sgroup(G, qg) + 1)
                    s.activation(s_tiles(qg), quad[:, :, 0:width(qg)], ACT.Copy).then_inc(s_free, 1)
                wait(act, s_free, b, 16, sgroup(G, QG - 1) + 1)
                for n in range(16):
                    qg = LO + n // 4
                    m = 32 * qg
                    src = s_tiles(qg)[:, n % 4, 0:m]
                    for a, func in enumerate((ACT.Copy, ACT.Square)):
                        step_n = 32 * G + 2 * n + a
                        wait(act, s_stats, b, 32 * NG, step_n - RING + 1)
                        s.activation(act_junk[:, step_n % RING, 0:m], src, func,
                                     accum_out=ssum[:, a, n:n + 1]).then_inc(s_stats, 1)

            def exps(b, G, qg):
                w = width(qg)
                if qg or G:
                    Bank(1, last_part(G, qg - 1) if qg else last_part(G - 1, QG - 1)).wait_read(act, b)
                wait(act, bmax_ready, b, 10, 5 * G + (1 if qg >= LO else qg + 2))
                lower = qg < LO
                if lower:
                    wait(act, s_full, b, 16, sgroup(G, qg) + 1)
                elif qg == LO:
                    wait(act, exact_done, b, NG, G + 1)
                for i in range(4):
                    src = quad[:, i, 0:w] if lower else s_tiles(qg)[:, i, :]
                    ins = s.activation(e_sb[:, i * w:(i + 1) * w], src, ACT.Exp, bias=bmax[:, qg, i:i + 1], scale=SCALE)
                ins.then_inc(s_free if lower else e_ready, 1)

            def p_out(b, G, qg):
                w = width(qg)
                if qg or G:
                    Bank(1, ("o", G, qg - 1) if qg else ("o", G - 1, QG - 1)).wait_full(act, b)
                for kb, rows in [(0, min(w, P))] + ([(1, w - P)] if w > P else []):
                    copy_out(1, ("pT", G, qg, kb), b, pT_sb[0:rows, kb, :], rows=rows)

            def norm_T(b, name, t, n):
                if n:
                    Bank(2, [("sim", 0), ("sim", 1), ("dense", 0, 1)][n - 1]).wait_full(act, b)
                for h in range(2):
                    copy_out(2, (name, t, h), b, nT[:, 4 * h:4 * h + 4, :].rearrange("p k n -> p (k n)"))

            def sim_exp(b, t):
                wait(act, smax_ready, b, NT, t + 1)
                bank = Bank(2, ("sim", t))
                bank.wait_full(act, b)
                s.activation(p2[:, t, :], bank.ps[:, 0:S], ACT.Exp, bias=small[:, 1:2], scale=XSCALE,
                             accum_out=small[:, 2:3]).then_inc(bank.free, 1)

            def gate_exp(b, t):
                wait(act, gmax_ready, b, NT, t + 1)
                bank = Bank(2, ("cent", t))
                bank.wait_full(act, b)
                s.activation(gate[:, 0, :], bank.ps[:, 0:NC], ACT.Exp, bias=small[:, 1:2], scale=10.0,
                             accum_out=small[:, 2:3]).then_inc(bank.free, 1)

            def stage2(b, G, k):
                if b is None:
                    return
                if G == 0 and k < NT:
                    norm_T(b, "nT", k, k)
                    sim_exp(b, k)
                elif G == 1 and k % 2 == 0:
                    norm_T(b, "mT", k // 2, NT + k // 2)
                    gate_exp(b, k // 2)

            def body(b, b2):
                normed_T(b)
                qkv(b)
                for G in range(NG):
                    upper_store(b, G)
                    for k in range(LO):
                        exps(b, G, k)
                        stage2(b2, G, k)
                        p_out(b, G, k)
                    for qg in range(LO, QG):
                        exps(b, G, qg)
                        p_out(b, G, qg)

            body(0, None)
            with act.Fori(1, B) as b:
                body(b, b - 1)
            for G in range(NG):
                for k in range(4):
                    stage2(B - 1, G, k)

        @block.gpsimd
        def _(pool):
            g = nc.gpsimd

            def power(b, n, per, got, made):
                wait(pool, got, b, per, n + 1)
                g.tensor_tensor(rstd[:, :], veps[:, :], half[:, 16:17], ALU.pow).then_inc(made, 1)

            def rope(b):
                for n in range(5):
                    Bank(1, ("q", n) if n < 4 else ("k",)).wait_read(pool, b)
                    wait(pool, qk_ready, b, 5, n)
                    g.tensor_tensor(q_cos[:, :].rearrange("p (a s) -> p a s", a=2), q_raw[:, :].rearrange("p (a s) -> p a s", a=2),
                                    cos_sin[:, 0:1, :].to_broadcast([P, 2, S]), ALU.mult).then_inc(q_cos_ready, 1)
                    wait(pool, q_cos_ready, b, 5, n + 1)
                    bank = Bank(1, ("rot", n))
                    bank.wait_read(pool, b)
                    if n < 4:
                        ra = 2 * (n % 2)
                        for a in range(2):
                            dst = qT[:, n // 2, :, (ra + a) * 32:(ra + a + 1) * 32]
                            ins = g.tensor_tensor(dst, q_cos[:, a * S:(a + 1) * S].rearrange("p (g q) -> p g q", q=32),
                                                  q_sin[:, a * S:(a + 1) * S].rearrange("p (g q) -> p g q", q=32), ALU.add)
                    else:
                        ins = g.tensor_tensor(kT[:, :, :].rearrange("p a s -> p (a s)"), q_cos[:, :], q_sin[:, :], ALU.add)
                    ins.then_inc(qk_ready, 1)

            def spread_of(b, G):
                wait(pool, var_s, b, NG, G + 1)
                g.tensor_tensor(sd[:, :], tmp[:, 1, :], half[:, 0:16], ALU.pow).then_inc(sd_ready, 1)

            def body(b, b2):
                for t in range(NT):
                    power(b, t, NT, var1, rstd1)
                if b2 is not None:
                    power(b2, 0, 2 * NT, var2, rstd2)
                rope(b)
                for G in range(NG):
                    spread_of(b, G)
                    if b2 is not None:
                        for n in ((1, 2), (3,))[G]:
                            power(b2, n, 2 * NT, var2, rstd2)

            pool.wait_ge(tables_in, 64)
            pool.wait_ge(consts_ready, 1)
            body(0, None)
            with pool.Fori(1, B) as b:
                body(b, b - 1)
            for n in range(2 * NT):
                power(B - 1, n, 2 * NT, var2, rstd2)
            pool.wait_ge(x2_out, 32 * B)
            pool.wait_ge(o_out, 16 * NT * B)
            pool.wait_ge(rows_ready, 1)
            rows_off = pool.value_load(flag_i[0:1, 0:1])
            with pool.If(rows_off > 0):
                with pool.Fori(0, B * NT) as n:
                    pool.dma_start(fix_a, out.rearrange("b (t p) d -> (b t) p d", p=P)[n]).then_inc(fix_in, 16)
                    pool.dma_start(fix_b, x2_dram.rearrange("b (t p) d -> (b t) p d", p=P)[n]).then_inc(fix_in, 16)
                    pool.wait_ge(fix_in, 32 * n + 32)
                    g.tensor_tensor(fix_a, fix_a, wo_sb[:, 0, :], ALU.mult)
                    g.tensor_tensor(fix_b, fix_b, wo_sb[:, 1, :], ALU.mult).then_inc(fix_step, 1)
                    pool.wait_ge(fix_step, 2 * n + 1)
                    g.tensor_tensor(fix_a, fix_a, fix_b, ALU.add).then_inc(fix_step, 1)
                    pool.wait_ge(fix_step, 2 * n + 2)
                    settle(pool)
                    pool.dma_start(out.rearrange("b (t p) d -> (b t) p d", p=P)[n], fix_a).then_inc(fix_out, 16)
                    pool.wait_ge(fix_out, 16 * n + 16)


CHAIN1 = 298
CHAIN2 = 18


def kernel(**inputs):
    import statistics
    import numpy as np
    import concourse.bacc as bacc
    from concourse.bass_utils import run_bass_kernel_spmd

    order = np.array([HD * (REP * (4 * G + i) + r) + d for G in range(NG) for r in range(REP) for i in range(4) for d in range(HD)])
    wq, wk, wv = (np.asarray(inputs[f"L0_attn_W{c}"]) for c in "qkv")
    wqkv = np.ascontiguousarray(np.concatenate([wq[order], wk, wv]).T)
    wo = np.ascontiguousarray(np.asarray(inputs["L0_attn_Wo"]).T[order])
    wf = np.ascontiguousarray(np.asarray(inputs["L0_ffn_weight"]).T)
    cent = np.ascontiguousarray(np.asarray(inputs["L0_ffn_centroids"]).T)
    ctx_kv = np.ascontiguousarray(inputs["ctx_4096"])
    ctx_t = np.ascontiguousarray(ctx_kv.transpose(0, 2, 1))
    assign = np.ascontiguousarray(np.broadcast_to(np.asarray(inputs["L0_ffn_assignments"]), (NC, D)))
    bias = np.ascontiguousarray(np.asarray(inputs["L0_ffn_bias"])[None, :])

    f32 = np.float32
    inv_freq = (f32(1.0) / np.power(f32(10000.0), np.arange(0, HD, 2, dtype=f32) / f32(HD))).astype(f32)
    angle = np.outer(np.arange(S, dtype=f32), inv_freq).astype(f32)
    channel = np.arange(P) % (HD // 2)
    tables = np.ascontiguousarray(np.stack([np.cos(angle).T[channel], np.sin(angle).T[channel]], axis=1).astype(f32))
    masks = np.zeros((P, 3 * P + 32), f32)
    row = np.arange(P)
    masks[row, row] = 1.0
    for m in range(P):
        if m % HD < HD // 2:
            masks[m + HD // 2, P + m] = -1.0
        else:
            masks[m - HD // 2, P + m] = 1.0
        masks[m, 2 * P + np.arange(REP) * 32 + m % 32] = 1.0
        masks[m, 3 * P + m % 32 + 1:] = NEG
    probe = np.zeros((P, 3 * 16 + 16 * WIN + 1), f32)
    normal = statistics.NormalDist()
    for n in range(16):
        qg = LO + n // 4
        for p in range(P):
            keys = 32 * qg + p % 32 + 1
            z = normal.inv_cdf(1 - TARGET / keys)
            probe[p, n] = z
            probe[p, 16 + n] = 1 / (keys * normal.pdf(z))
            probe[p, 32 + n] = 1 / (32 * qg)
        probe[:, 48 + n * WIN:48 + (n + 1) * WIN] = np.arange(WIN)
    probe[:, -1] = np.arange(P)

    arrays = dict(x=np.ascontiguousarray(inputs["x"]), ctx_kv=ctx_kv, ctx_t=ctx_t, wqkv=wqkv, wo=wo, wf=wf, cent=cent,
                  bias=bias, assign=assign, tables=tables, masks=masks, probe=probe)
    nc = bacc.Bacc("TRN2", target_bir_lowering=False, num_devices=1)
    args = [nc.dram_tensor(f"in_{k}", a.shape, mybir.dt.from_np(a.dtype), kind="ExternalInput").ap() for k, a in arrays.items()]
    out = nc.dram_tensor("out_0", (B, S, D), F32, kind="ExternalOutput").ap()
    x2_dram = nc.dram_tensor("x2_dram", (B, S, D), F32).ap()
    build(nc, *args, out, x2_dram)
    got = run_bass_kernel_spmd(nc, [{f"in_{k}": a for k, a in arrays.items()}], core_ids=[0])
    return got.results[0]["out_0"]
```

```python
from contextlib import ExitStack

import concourse.bass as bass
from concourse import mybir

ALU = mybir.AluOpType
ACT = mybir.ActivationFunctionType
AX = mybir.AxisListType
F32 = mybir.dt.float32
I32 = mybir.dt.int32
BF16 = mybir.dt.bfloat16

P = 128
B, S, D = 8, 256, 1024
H, HKV, HD = 32, 8, 32
REP = H // HKV
KT_ = D // P
NT = S // P
NG = HKV // 4
WG = 6 * P
QG = S // 32
KEEP = 128
LO = KEEP // 32
NC = 64
SCALE = float(HD) ** -0.5
XSCALE = float(S) ** -0.5
EPS = 1e-5
NEG = -2.0 ** 100
WIN = 8
TARGET = KEEP - (WIN - 1) / 2
RING = 3
COUNTS = 4
DAMP = 0.9


def width(qg):
    return 32 * (qg + 1)


HOFF = [0]
for _g in range(LO, QG):
    HOFF.append(HOFF[-1] + 4 * width(_g))


def attention_jobs():
    jobs = []
    for G in range(NG):
        for qg in range(LO):
            jobs += [("pT", G, qg, 0), ("o", G, qg)]
        jobs.append(("flag", G))
        for qg in range(LO, QG):
            jobs += [("pT", G, qg, 0), ("pT", G, qg, 1), ("o", G, qg)]
    assert len(jobs) % 2 == 0
    return jobs


STEPS = {
    (0, 0): [("wo", -1, 0, 0), ("wo", -1, 0, 1), ("wo", -1, 1, 0)],
    (0, 1): [("wo", -1, 1, 1), ("ln2", -1, 0), ("kv", 0, 1), ("rot", 0, 1, 0)],
    (0, 2): [("nT", -1, 0), ("q", 0, 1, 0), ("sim", -1, 0), ("rot", 0, 1, 1), ("ln2", -1, 1)],
    (0, 3): [("q", 0, 1, 1), ("nT", -1, 1), ("sim", -1, 1), ("rot", 0, 1, 2)],
    (0, 4): [("flag", 0, 0), ("ctx", -1, 0)],
    (0, 5): [("ctx", -1, 1), ("ln1", 1, 0)],
    (0, 6): [("xT", 1, 0), ("ln1", 1, 1)],
    (0, 7): [("xT", 1, 1), ("ln2", -1, 2)],
    (1, 0): [("kv", 1, 0), ("mT", -1, 0), ("q", 1, 0, 0), ("rot", 1, 0, 0), ("cent", -1, 0)],
    (1, 1): [("rot", 1, 0, 1), ("q", 1, 0, 1)],
    (1, 2): [("rot", 1, 0, 2), ("dense", -1, 0, 0), ("ln2", -1, 3)],
    (1, 3): [("dense", -1, 0, 1)],
    (1, 4): [("mT", -1, 1), ("cent", -1, 1), ("flag", 0, 1), ("dense", -1, 1, 0)],
    (1, 5): [("dense", -1, 1, 1)],
}
PROLOGUE = [("xT", 0, 0), ("xT", 0, 1), ("kv", 0, 0), ("rot", 0, 0, 0), ("q", 0, 0, 0), ("rot", 0, 0, 1), ("q", 0, 0, 1), ("rot", 0, 0, 2)]


def steps_of(kind, G, k):
    batches = {"first": (0, 1), "loop": (-1, 0, 1), "last": (-1, 0), "tail": (-1,)}[kind]
    return [piece for piece in STEPS.get((G, k), []) if piece[1] in batches]


def dense_jobs(pieces):
    jobs = []
    for piece in pieces:
        if piece[0] in ("xT", "nT", "mT", "ctx"):
            jobs += [piece + (h,) for h in range(2)]
        elif piece[0] not in ("ln1", "ln2", "flag"):
            jobs.append(piece)
    return jobs


def build(nc, x, ctx_kv, ctx_t, wqkv, wo, wf, cent, bias, assign, tables, masks, probe, out, x2_dram):
    with ExitStack() as st:
        def sb(name, shape, dt=F32):
            return st.enter_context(nc.sbuf_tensor(name, shape, dt))

        def sem(name):
            return st.enter_context(nc.semaphore(name))

        wqkv_sb = sb("wqkv_sb", [P, KT_, D + 2 * HKV * HD])
        wo_sb = sb("wo_sb", [P, KT_, D])
        wf_sb = sb("wf_sb", [P, KT_, D])
        cent_sb = sb("cent_sb", [P, KT_, NC])
        cos_sin = sb("cos_sin", [P, 2, S])
        mask_sb = sb("mask_sb", [P, 3 * P + 32])
        ident, rotate, spread = (mask_sb[:, j * P:(j + 1) * P] for j in range(3))
        future = mask_sb[:, 3 * P:3 * P + 32]
        row_sb = sb("row_sb", [P, 3 * 16 + 16 * WIN + 1])
        probe_sb = row_sb[:, 0:48].rearrange("p (a n) -> p a n", a=3)
        iota8 = row_sb[:, 48:48 + 16 * WIN].rearrange("p (a n) -> p a n", a=16)
        cluster_id = row_sb[:, 48 + 16 * WIN:]
        ones = sb("ones", [P, P])
        bias_sb = sb("bias_sb", [P, KT_])
        half = sb("half", [P, 32])
        x_sb = sb("x_sb", [P, NT, D])
        e_sb = sb("e_sb", [P, 2, 4 * S])
        pT_sb = sb("pT_sb", [P, 2, 4 * P])
        xn = sb("xn", [P, D])
        xT = sb("xT", [P, KT_, S])
        oT = sb("oT", [P, KT_, S])
        qT = sb("qT", [P, NG, QG, REP * 32])
        kT = sb("kT", [P, NG, S])
        v_sb = sb("v_sb", [P, NT, HKV * HD])
        q_raw = sb("q_raw", [P, 2, 2 * S])
        q_sin = sb("q_sin", [P, 2 * S])
        below = sb("below", [P, RING, S])
        s_sb = sb("s_sb", [P, HOFF[-1]])
        hit = sb("hit", [P, RING, S], BF16)
        act_junk = sb("act_junk", [P, 2, S], BF16)
        o_scale = sb("o_scale", [P, P])
        rsum = sb("rsum", [P, 2, 4])
        rinv = sb("rinv", [P, 2, 4])
        ssum = sb("ssum", [P, 2, 16])
        nmax = sb("nmax", [P, QG, 4])
        bmax = sb("bmax", [P, QG, 4])
        tq = sb("tq", [P, 2, 16])
        dq = sb("dq", [P, 2, 16])
        sd = sb("sd", [P, 16])
        step = sb("step", [P, 3, 16])
        tmp = sb("tmp", [P, 4, 16])
        cand = sb("cand", [P, 16, WIN + 1])
        pick, prod = (below[:, j, 0:16 * WIN].rearrange("p (a n) -> p a n", a=16) for j in range(2))
        thr = sb("thr", [P, 2, 16])
        fail = sb("fail", [P, 16])
        flag_f = sb("flag_f", [1, 21])
        flag_i = sb("flag_i", [1, 21], I32)
        top8 = sb("top8", [P, 8])
        stats = sb("stats", [P, 12])
        mv = sb("mv", [P, 2])
        rstd = sb("rstd", [P, 1])
        veps = sb("veps", [P, 1])
        x1 = sb("x1", [P, NT, D])
        nT = sb("nT", [P, KT_, P])
        ctx_sb = sb("ctx_sb", [P, NT * D])
        ctxT_sb = ctx_sb[:, :].rearrange("p (k s) -> p k s", k=KT_)
        ctxv_sb = ctx_sb[:, :].rearrange("p (t d) -> p t d", t=NT)
        p2 = sb("p2", [P, NT, S])
        small = sb("small", [P, 4])
        picked = sb("picked", [P, NT])
        gate = sb("gate", [P, 2, NC])
        hits = sb("hits", [P, NC])

        assign_sb = xT[0:NC, 0:4, :].rearrange("p k n -> p (k n)").bitcast(I32)
        one_hot = s_sb[0:NC, 0:D]
        row_on = wo_sb[:, 0, :].rearrange("p (h n) -> p h n", h=2)
        row_off = wo_sb[:, 1, :].rearrange("p (h n) -> p h n", h=2)
        fix_a, fix_b = wo_sb[:, 2, :], wo_sb[:, 3, :]

        quad = st.enter_context(nc.psum_tensor("quad", [P, 4, 512], F32))
        acc1 = [st.enter_context(nc.psum_tensor(f"acc1_{j}", [P, 512], F32)) for j in range(2)]
        acc2 = [st.enter_context(nc.psum_tensor(f"acc2_{j}", [P, 512], F32)) for j in range(2)]

        tables_in, wqkv_in, wo_in, wf_in, consts_ready = map(sem, ("tables_in", "wqkv_in", "wo_in", "wf_in", "consts_ready"))
        x_in, xres_in, ctxT_in, ctxv_in = map(sem, ("x_in", "xres_in", "ctxT_in", "ctxv_in"))
        full1 = [sem(f"full1_{j}") for j in range(2)]
        free1 = [sem(f"free1_{j}") for j in range(2)]
        full2 = [sem(f"full2_{j}") for j in range(2)]
        free2 = [sem(f"free2_{j}") for j in range(2)]
        var1, rstd1, xn1, ln1_step = sem("var1"), sem("rstd1"), sem("xn1"), sem("ln1_step")
        var2, rstd2, xn2, ln2_step = sem("var2"), sem("rstd2"), sem("xn2"), sem("ln2_step")
        q_cos_ready, qk_ready = sem("q_cos_ready"), sem("qk_ready")
        s_full, s_free, s_stats = sem("s_full"), sem("s_free"), sem("s_stats")
        var_s, sd_ready = sem("var_s"), sem("sd_ready")
        bmax_ready, e_ready, p_ready, fail_ready, exact_done = map(
            sem, ("bmax_ready", "e_ready", "p_ready", "fail_ready", "exact_done"))
        x2_out, o_out, smax_ready, p2_ready, gmax_ready = map(
            sem, ("x2_out", "o_out", "smax_ready", "p2_ready", "gmax_ready"))
        select_step, stage2_step = sem("select_step"), sem("stage2_step")
        passed = sem("passed")
        fin_sel, fin_pe, fin_step, rows_ready, fix_in, fix_step, fix_out, cluster_ready, assign_in = map(
            sem, ("fin_sel", "fin_pe", "fin_step", "rows_ready", "fix_in", "fix_step", "fix_out", "cluster_ready", "assign_in"))

        at1 = {j: (n % 2, n // 2) for n, j in enumerate(attention_jobs())}
        N1 = len(attention_jobs()) // 2
        pro = dense_jobs(PROLOGUE)
        seqs = {kind: [j for G in range(NG) for k in range(QG) for j in dense_jobs(steps_of(kind, G, k))]
                for kind in ("first", "loop", "last", "tail")}
        base_first = len(pro)
        base_loop = base_first + len(seqs["first"])
        N2 = len(seqs["loop"])
        base_last = base_loop + (B - 2) * N2
        base_tail = base_last + len(seqs["last"])
        assert base_loop % 2 == 0 and N2 % 2 == 0
        base = {"pro": 0, "first": base_first, "last": base_last, "tail": base_tail}
        seqs["pro"] = pro

        def wait(eng, s, b, per, k):
            v = b * per + k
            if isinstance(v, int) and v <= 0:
                return
            eng.wait_ge(s, v)

        def settle(eng):
            eng.sem_inc(passed, 1)

        class Turn:
            def wait_free(self, eng):
                wait(eng, self.free, self.b, self.per, self.n)

            def wait_read(self, eng):
                wait(eng, self.free, self.b, self.per, self.n + 1)

            def wait_full(self, eng):
                wait(eng, self.full, self.b, self.per, self.n + 1)

        class Attn(Turn):
            def __init__(self, b, *job):
                j, self.n = at1[job]
                self.b, self.per = b, N1
                self.ps, self.full, self.free = acc1[j], full1[j], free1[j]

        class Dense(Turn):
            def __init__(self, kind, b, *job):
                at = seqs[kind].index(job)
                if kind == "loop":
                    at += base_loop
                    self.b, self.per, self.n = b - 1, N2 // 2, at // 2
                else:
                    at += base[kind]
                    self.b, self.per, self.n = 0, 0, at // 2
                j = at % 2
                self.ps, self.full, self.free = acc2[j], full2[j], free2[j]

        def upper_group(b, G, qg):
            return b, 8 * G + qg - LO

        def lower_group(b, G, k):
            return b, 8 * G + LO + k

        def s_tiles(qg):
            o = HOFF[qg - LO]
            return s_sb[:, o:o + 4 * width(qg)].rearrange("p (i w) -> p i w", i=4)

        def parts(qg):
            w = width(qg)
            return [(0, min(w, P))] + ([(1, w - P)] if w > P else [])

        block = st.enter_context(nc.Block())

        def pieces(table, kind, b, G, k):
            for name, db, *args in steps_of(kind, G, k):
                if name in table:
                    table[name](kind, b, db, *args)

        @block.sync
        def _(sp):
            def load_x(b):
                wait(sp, xn1, b, NT, 0)
                sp.dma_start(x_sb[:, :, :], x[b].rearrange("(t p) d -> p t d", p=P)).then_inc(x_in, 16)

            def load_next(b):
                sp.dma_start(ctxT_sb, ctx_t[b].rearrange("(k p) s -> p k s", p=P)).then_inc(ctxT_in, 16)
                wait(sp, o_out, b, 16 * NT, 0)
                sp.dma_start(x1[:, :, :], x[b].rearrange("(t p) d -> p t d", p=P)).then_inc(xres_in, 16)

            def layers_of(kind, b, pb):
                Dense(kind, b, "sim", -1, NT - 1).wait_full(sp)
                sp.dma_start(ctxv_sb, ctx_kv[pb].rearrange("(t p) d -> p t d", p=P)).then_inc(ctxv_in, 16)
                for t in range(NT):
                    Dense(kind, b, "ctx", -1, t, 1).wait_read(sp)
                    sp.dma_start(x2_dram[pb, t * P:(t + 1) * P, :], x1[:, t, :]).then_inc(x2_out, 16)
                for t in range(NT):
                    Dense(kind, b, "dense", -1, t, 1).wait_read(sp)
                    sp.dma_start(out[pb, t * P:(t + 1) * P, :], x1[:, t, :]).then_inc(o_out, 16)

            wq_part = wqkv.rearrange("(k p) n -> p k n", p=P)
            sp.dma_start(row_sb[:, :], probe).then_inc(tables_in, 16)
            sp.dma_start(mask_sb[:, :], masks).then_inc(tables_in, 16)
            load_x(0)
            sp.dma_start(cos_sin[:, :, :], tables).then_inc(tables_in, 16)
            sp.dma_start(bias_sb[:, :], bias).then_inc(tables_in, 16)
            sp.dma_start(wqkv_sb[:, :, 0:WG], wq_part[:, :, 0:WG]).then_inc(wqkv_in, 16)
            sp.dma_start(wqkv_sb[:, :, WG:], wq_part[:, :, WG:]).then_inc(wqkv_in, 16)
            load_x(1)
            load_next(0)
            sp.dma_start(wo_sb[:, :, :], wo.rearrange("(k p) n -> p k n", p=P)).then_inc(wo_in, 16)
            sp.dma_start(cent_sb[:, :, :], cent.rearrange("(k p) n -> p k n", p=P)).then_inc(wf_in, 16)
            sp.dma_start(wf_sb[:, :, :], wf.rearrange("(k p) n -> p k n", p=P)).then_inc(wf_in, 16)
            with sp.Fori(1, B - 1) as b:
                load_x(b + 1)
                layers_of("loop", b, b - 1)
                load_next(b)
            layers_of("last", B - 1, B - 2)
            load_next(B - 1)
            Dense("last", B - 1, "kv", 0, 1).wait_full(sp)
            sp.dma_start(assign_sb, assign).then_inc(assign_in, 16)
            layers_of("tail", B, B - 1)
            sp.wait_ge(x2_out, 16 * NT * B)
            sp.wait_ge(o_out, 16 * NT * B)

        @block.tensor
        def _(pe):
            def begin(turn):
                turn.wait_free(pe)
                return turn

            def product(dst, lhs, rhs, steps=KT_):
                for k in range(steps):
                    mm = pe.matmul(dst, lhs(k), rhs(k), start=(k == 0), stop=(k == steps - 1))
                return mm

            def tile_T(turn, h):
                begin(turn)
                for j in range(4):
                    mm = pe.transpose(turn.ps[:, j * P:(j + 1) * P], xn[:, (4 * h + j) * P:(4 * h + j + 1) * P], ident)
                mm.then_inc(turn.full, 1)

            def x_T(kind, b, db, t):
                wait(pe, xn1, b + db, NT, t + 1)
                for h in range(2):
                    tile_T(Dense(kind, b, "xT", db, t, h), h)

            def q_pair(kind, b, db, G, n):
                turn = begin(Dense(kind, b, "q", db, G, n))
                for a in range(2):
                    c = G * WG + (2 * n + a) * P
                    mm = product(turn.ps[:, a * S:(a + 1) * S], lambda k: wqkv_sb[:, k, c:c + P], lambda k: xT[:, k, :])
                mm.then_inc(turn.full, 1)

            def keys_values(kind, b, db, G):
                if G == 0:
                    Dense(kind, b, "xT", db, NT - 1, 1).wait_read(pe)
                c = G * WG + 4 * P
                turn = begin(Dense(kind, b, "kv", db, G))
                product(turn.ps[:, 0:S], lambda k: wqkv_sb[:, k, c:c + P], lambda k: xT[:, k, :])
                for t in range(NT):
                    mm = product(turn.ps[:, S + t * P:S + (t + 1) * P], lambda k: xT[:, k, t * P:(t + 1) * P],
                                 lambda k: wqkv_sb[:, k, c + P:c + 2 * P])
                mm.then_inc(turn.full, 1)

            def rot(kind, b, db, G, m):
                src = Dense(kind, b, "q", db, G, m - 1) if m else Dense(kind, b, "kv", db, G)
                src.wait_read(pe)
                cols = 2 * S if m else S
                turn = begin(Dense(kind, b, "rot", db, G, m))
                pe.matmul(turn.ps[:, 0:cols], rotate, q_raw[:, m % 2, 0:cols], start=True, stop=True).then_inc(turn.full, 1)

            def scores(group, G, qg):
                b, n = group
                wait(pe, s_free, b, 16, n)
                w = width(qg)
                for i in range(4):
                    r = slice(32 * i, 32 * i + 32)
                    pe.matmul(quad[:, i, 0:w], qT[r, G, qg, :], kT[r, G, 0:w], start=True, stop=False, skip_group_check=True)
                for i in range(4):
                    r = slice(32 * i, 32 * i + 32)
                    mm = pe.matmul(quad[:, i, w - 32:w], spread[r, :], future[r, :],
                                   start=False, stop=True, skip_group_check=True)
                mm.then_inc(s_full, 1)

            def upper_scores(b, G, qg):
                if qg == LO:
                    wait(pe, qk_ready, b, 6, 3 * G + 3)
                scores(upper_group(b, G, qg), G, qg)

            def weights_T(b, G, qg):
                w = width(qg)
                if qg < LO:
                    pb, n = lower_group(b, G, qg)
                    wait(pe, s_free, pb, 16, n + 1)
                else:
                    wait(pe, p_ready, b, 16, 8 * G + qg + 1)
                for kb, rows in parts(qg):
                    turn = begin(Attn(b, "pT", G, qg, kb))
                    settle(pe)
                    for i in range(4):
                        o = i * w + kb * P
                        mm = pe.transpose(turn.ps[0:rows, i * P:(i + 1) * P], e_sb[:, qg % 2, o:o + rows], ident)
                    mm.then_inc(turn.full, 1)

            def values(b, G, qg):
                turn = begin(Attn(b, "o", G, qg))
                Attn(b, "pT", G, qg, len(parts(qg)) - 1).wait_read(pe)
                settle(pe)
                for i in range(4):
                    kv = 4 * G + i
                    for kb, rows in parts(qg):
                        pe.matmul(turn.ps[32 * i:32 * i + 32, 0:P], v_sb[0:rows, kb, kv * HD:(kv + 1) * HD],
                                  pT_sb[0:rows, kb, i * P:(i + 1) * P], start=(kb == 0), stop=True, skip_group_check=True)
                wait(pe, p_ready, b, 16, 8 * G + qg + 1)
                for i in range(4):
                    mm = pe.matmul(turn.ps[32 * i:32 * i + 32, P:2 * P], rinv[:, qg % 2, i:i + 1].to_broadcast([P, 32]),
                                   ident, start=False, stop=True, skip_group_check=True)
                mm.then_inc(turn.full, 1)

            def out_proj(kind, b, db, t, h):
                if h == 0:
                    Attn(b - 1, "o", NG - 1, LO - 1 if t == 0 else QG - 1).wait_read(pe)
                if kind == "loop" and (t, h) == (0, 0):
                    pe.wait_ge(wo_in, 16)
                turn = begin(Dense(kind, b, "wo", -1, t, h))
                product(turn.ps[:, :], lambda k: oT[:, k, t * P:(t + 1) * P],
                        lambda k: wo_sb[:, k, h * 512:(h + 1) * 512]).then_inc(turn.full, 1)

            def n_T(kind, b, db, t):
                wait(pe, xn2, b - 1, 2 * NT, t + 1)
                for h in range(2):
                    tile_T(Dense(kind, b, "nT", -1, t, h), h)

            def m_T(kind, b, db, t):
                wait(pe, xn2, b - 1, 2 * NT, NT + t + 1)
                for h in range(2):
                    tile_T(Dense(kind, b, "mT", -1, t, h), h)

            def sim(kind, b, db, t):
                Dense(kind, b, "nT", -1, t, 1).wait_read(pe)
                if t == 0:
                    wait(pe, ctxT_in, b - 1, 16, 16)
                turn = begin(Dense(kind, b, "sim", -1, t))
                product(turn.ps[:, 0:S], lambda k: nT[:, k, :], lambda k: ctxT_sb[:, k, :]).then_inc(turn.full, 1)

            def context(kind, b, db, c):
                if c == 0:
                    wait(pe, p2_ready, b - 1, NT, NT)
                    wait(pe, ctxv_in, b - 1, 16, 16)
                for h in range(2):
                    turn = begin(Dense(kind, b, "ctx", -1, c, h))
                    product(turn.ps[:, :], lambda k: p2[:, k, c * P:(c + 1) * P],
                            lambda k: ctxv_sb[:, k, h * 512:(h + 1) * 512], NT).then_inc(turn.full, 1)

            def gate_logits(kind, b, db, t):
                if kind == "loop" and t == 0:
                    pe.wait_ge(wf_in, 32)
                Dense(kind, b, "mT", -1, t, 1).wait_read(pe)
                turn = begin(Dense(kind, b, "cent", -1, t))
                product(turn.ps[:, 0:NC], lambda k: nT[:, k, :], lambda k: cent_sb[:, k, :]).then_inc(turn.full, 1)

            def dense(kind, b, db, t, h):
                turn = begin(Dense(kind, b, "dense", -1, t, h))
                for j in range(4):
                    pe.matmul(turn.ps[:, j * P:(j + 1) * P], bias_sb[:, 4 * h + j:4 * h + j + 1].to_broadcast([P, P]),
                              ident, start=(j == 0), stop=False, skip_group_check=True)
                for k in range(KT_):
                    mm = pe.matmul(turn.ps[:, :], nT[:, k, :], wf_sb[:, k, h * 512:(h + 1) * 512],
                                   start=False, stop=(k == KT_ - 1), skip_group_check=True)
                mm.then_inc(turn.full, 1)

            def flags(kind, b, db, G):
                turn = begin(Attn(b, "flag", G))
                wait(pe, fail_ready, b, NG, G + 1)
                pe.matmul(turn.ps[0:1, 0:16], ones[:, 0:1], fail[:, :], start=True, stop=True).then_inc(turn.full, 1)

            table = dict(flag=flags, xT=x_T, q=q_pair, kv=keys_values, rot=rot, wo=out_proj, nT=n_T, mT=m_T, sim=sim,
                         ctx=context, cent=gate_logits, dense=dense)

            def body(kind, b):
                for G in range(NG):
                    scores(lower_group(b, G, 0), G, 0)
                    for k in range(LO):
                        pieces(table, kind, b, G, k)
                        weights_T(b, G, k)
                        if k + 1 < LO:
                            scores(lower_group(b, G, k + 1), G, k + 1)
                        values(b, G, k)
                    for qg in range(LO, QG):
                        pieces(table, kind, b, G, qg)
                        weights_T(b, G, qg)
                        if G == 0:
                            upper_scores(b, 1, qg)
                        elif kind != "last":
                            upper_scores(b + 1, 0, qg)
                        values(b, G, qg)

            pe.wait_ge(tables_in, 64)
            pe.wait_ge(consts_ready, 1)
            for name, *args in PROLOGUE:
                if name == "kv":
                    pe.wait_ge(wqkv_in, 32)
                table[name]("pro", 0, *args)
            for qg in range(LO, QG):
                upper_scores(0, 0, qg)
            body("first", 0)
            with pe.Fori(1, B - 1) as b:
                body("loop", b)
            body("last", B - 1)
            for G in range(NG):
                for k in range(QG):
                    pieces(table, "tail", B, G, k)
            pe.wait_ge(fin_sel, 1)
            pe.matmul(quad[0:NC, 0, 0:1], hits[:, :], ones[:, 0:1], start=True, stop=True).then_inc(fin_pe, 1)
            pe.wait_ge(cluster_ready, 1)
            for h in range(2):
                mm = pe.matmul(quad[:, h + 1, :], e_sb[0:NC, 0, 0:P], one_hot[:, h * 512:(h + 1) * 512], start=True, stop=True)
            mm.then_inc(fin_pe, 1)

        @block.vector
        def _(dve):
            v = nc.vector

            class Chain:
                def __init__(self, s, per):
                    self.s, self.per, self.b, self.k = s, per, 0, 0

                def start(self, b, k=0):
                    self.b, self.k = b, k

                def put(self, ins):
                    self.k += 1
                    ins.then_inc(self.s, 1)
                    return self.k

                def upto(self, k, apart=False):
                    wait(dve, self.s, self.b, self.per, k)
                    if apart:
                        settle(dve)

                def __call__(self, ins, apart=False):
                    self.upto(self.put(ins), apart)

            c1, c2 = Chain(select_step, CHAIN1), Chain(stage2_step, CHAIN2)
            n1, n2 = Chain(ln1_step, 2 * NT), Chain(ln2_step, 4 * NT)

            v.memset(ones[:, :], 1.0)
            v.memset(hits[:, :], 0.0)
            v.memset(half[:, 0:16], 0.5)
            v.memset(half[:, 16:32], -0.5).then_inc(consts_ready, 1)
            dve.wait_ge(consts_ready, 1)
            dve.wait_ge(tables_in, 64)

            def layer_norm(b, n, per, src, link, var_sem, rstd_sem, xn_sem, xn_free):
                link.start(b, 2 * n)
                for h in range(2):
                    ins = v.bn_stats(stats[:, 6 * h:6 * h + 6], src[:, h * 512:(h + 1) * 512])
                link(ins, apart=True)
                link(v.bn_aggr(mv[:, :], stats[:, :]))
                v.tensor_scalar(veps[:, :], mv[:, 1:2], EPS, None, ALU.add).then_inc(var_sem, 1)
                if xn_free:
                    xn_free.wait_full(dve)
                wait(dve, rstd_sem, b, per, n + 1)
                v.tensor_scalar(xn[:, :], src, mv[:, 0:1], rstd[:, 0:1], ALU.subtract, ALU.mult).then_inc(xn_sem, 1)

            def ln1(b, t, xn_free):
                if t == 0:
                    wait(dve, x_in, b, 16, 16)
                layer_norm(b, t, NT, x_sb[:, t, :], n1, var1, rstd1, xn1, xn_free)

            def ln2(b, n, xn_free):
                layer_norm(b, n, 2 * NT, x1[:, n % NT, :], n2, var2, rstd2, xn2, xn_free)

            def later_norm(kind, b, db, n):
                free = None
                if n % 2:
                    free = Dense(kind, b, "nT" if n < 2 else "mT", -1, 0, 1)
                elif n == 2:
                    free = Dense(kind, b, "xT", 1, NT - 1, 1) if kind == "loop" else Dense(kind, b, "nT", -1, 1, 1)
                ln2(b - 1, n, free)

            def first_norm(kind, b, db, t):
                if t:
                    free = Dense(kind, b, "xT", db, 0, 1)
                else:
                    free = Dense(kind, b, "nT", -1, 1, 1) if kind == "loop" else None
                ln1(b + db, t, free)

            def rotary(kind, b, db, G, m):
                turn = Dense(kind, b, "rot", db, G, m)
                turn.wait_full(dve)
                wait(dve, qk_ready, b + db, 6, 3 * G + m)
                if m:
                    v.tensor_tensor(q_sin[:, :].rearrange("p (a s) -> p a s", a=2), turn.ps[:, :].rearrange("p (a s) -> p a s", a=2),
                                    cos_sin[:, 1:2, :].to_broadcast([P, 2, S]), ALU.mult).then_inc(turn.free, 1)
                else:
                    v.tensor_tensor(q_sin[:, 0:S], turn.ps[:, 0:S], cos_sin[:, 1, :], ALU.mult).then_inc(turn.free, 1)

            def tile(n):
                return s_tiles(LO + n // 4)[:, n % 4, :]

            def upper_setup(b, G):
                for qg in range(LO, QG):
                    pb, n = upper_group(b, G, qg)
                    wait(dve, s_free, pb, 16, n + 1)
                    ins = v.tensor_reduce(nmax[:, qg, :], s_tiles(qg), AX.X, ALU.max, negate=True)
                c1(ins)
                v.tensor_scalar(bmax[:, LO:, :], nmax[:, LO:, :], SCALE, None, ALU.mult).then_inc(bmax_ready, 1)
                wait(dve, s_stats, b, 32 * NG, 32 * G + 32)
                mu, ex2 = ssum[:, 0, :], ssum[:, 1, :]
                v.tensor_tensor(tmp[:, 0, :], mu, probe_sb[:, 2, :], ALU.mult)
                c1(v.tensor_tensor(tmp[:, 1, :], ex2, probe_sb[:, 2, :], ALU.mult))
                c1(v.tensor_tensor(tmp[:, 2, :], tmp[:, 0, :], tmp[:, 0, :], ALU.mult))
                c1(v.tensor_tensor(tmp[:, 1, :], tmp[:, 1, :], tmp[:, 2, :], ALU.subtract))
                v.tensor_scalar(tmp[:, 1, :], tmp[:, 1, :], 1e-30, None, ALU.max).then_inc(var_s, 1)

            def first_threshold(b, G):
                wait(dve, sd_ready, b, NG, G + 1)
                c1(v.tensor_tensor(tmp[:, 2, :], sd[:, :], probe_sb[:, 0, :], ALU.mult))
                v.tensor_tensor(tq[:, 0, :], tmp[:, 0, :], tmp[:, 2, :], ALU.add)
                c1(v.tensor_tensor(step[:, 0, :], sd[:, :], probe_sb[:, 1, :], ALU.mult))
                v.tensor_scalar(step[:, 1, :], step[:, 0, :], 1 / 3, None, ALU.mult)
                c1(v.tensor_scalar(step[:, 2, :], step[:, 0, :], 10 / 3, None, ALU.mult))

            def count(k, between):
                new = k % 2
                counted, lowered, listed = [], [], []

                def count_tile(n):
                    w = width(LO + n // 4)
                    if n >= RING:
                        c1.upto((lowered if k == COUNTS - 1 else counted)[n - RING])
                    counted.append(c1.put(v.tensor_scalar(hit[:, n % RING, 0:w], tile(n), tq[:, new, n:n + 1], -TARGET,
                                                          ALU.is_ge, ALU.add, accum_out=dq[:, new, n:n + 1])))

                def lower_tile(n):
                    w = width(LO + n // 4)
                    c1.upto(max(counted[n], listed[n - RING] if n >= RING else 0))
                    lowered.append(c1.put(v.scalar_tensor_tensor(below[:, n % RING, 0:w], hit[:, n % RING, 0:w], NEG, tile(n),
                                                                 ALU.mult, ALU.add)))

                def list_tile(n):
                    w = width(LO + n // 4)
                    c1.upto(lowered[n], apart=True)
                    listed.append(c1.put(v.max(cand[:, n, 1:WIN + 1], below[:, n % RING, 0:w])))

                for n in range(16 + (2 if k == COUNTS - 1 else 0)):
                    if n in between:
                        between[n]()
                    if n < 16:
                        count_tile(n)
                    if k == COUNTS - 1:
                        if 1 <= n <= 16:
                            lower_tile(n - 1)
                        if n >= 2:
                            list_tile(n - 2)
                c1.upto(c1.k)

            def update(k):
                new, old = k % 2, (k + 1) % 2
                t, d = tq[:, new, :], dq[:, new, :]
                slope = step[:, 0, :]
                if k:
                    slope = tmp[:, 0, :]
                    v.tensor_tensor(tmp[:, 1, :], dq[:, old, :], d, ALU.subtract)
                    c1(v.tensor_tensor(tmp[:, 0, :], t, tq[:, old, :], ALU.subtract))
                    v.tensor_tensor(tmp[:, 0, :], tmp[:, 0, :], tmp[:, 1, :], ALU.mult)
                    c1(v.tensor_tensor(tmp[:, 2, :], tmp[:, 1, :], tmp[:, 1, :], ALU.mult))
                    c1(v.tensor_scalar(tmp[:, 2, :], tmp[:, 2, :], 1.0, None, ALU.max))
                    c1(v.reciprocal(tmp[:, 1, :], tmp[:, 2, :]))
                    c1(v.tensor_tensor(tmp[:, 2, :], tmp[:, 0, :], tmp[:, 1, :], ALU.mult))
                    c1(v.tensor_tensor(tmp[:, 1, :], tmp[:, 2, :], step[:, 1, :], ALU.max))
                    v.tensor_tensor(tmp[:, 0, :], tmp[:, 1, :], step[:, 2, :], ALU.min)
                c1(v.tensor_tensor(tmp[:, 3, :], d, d, ALU.mult))
                c1(v.scalar_tensor_tensor(tmp[:, 3, :], tmp[:, 3, :], 13.0, d, ALU.is_gt, ALU.mult))
                c1(v.tensor_tensor(tmp[:, 3, :], tmp[:, 3, :], slope, ALU.mult))
                c1(v.tensor_tensor(tq[:, old, :], t, tmp[:, 3, :], ALU.add))

            def select(b, G):
                last = (COUNTS - 1) % 2
                v.tensor_copy(cand[:, :, 0:1], tq[:, last, :].rearrange("p (n o) -> p n o", o=1))
                c1(v.tensor_scalar(tmp[:, 0, :], dq[:, last, :], -1.0, (WIN - 1) / 2, ALU.mult, ALU.add))
                c1(v.tensor_tensor(pick[:, :, :], iota8[:, :, :],
                                   tmp[:, 0, :].rearrange("p (n o) -> p n o", o=1).to_broadcast([P, 16, WIN]), ALU.is_equal))
                for m in range(2):
                    c1(v.tensor_tensor(prod[:, :, :], pick[:, :, :], cand[:, :, m:m + WIN], ALU.mult))
                    c1(v.tensor_reduce(thr[:, m, :], prod[:, :, :], AX.X, ALU.add))
                v.tensor_tensor(fail[:, :], thr[:, 0, :], thr[:, 1, :], ALU.is_equal).then_inc(fail_ready, 1)

            def exact_tile(n):
                w = width(LO + n // 4)
                left, drop = below[:, 0, 0:w], below[:, 1, 0:w]
                v.tensor_copy(left, tile(n))
                dve.drain()
                with dve.Fori(0, KEEP // 8) as _r:
                    v.max(top8[:, :], left)
                    dve.drain()
                    v.match_replace(left, top8[:, :], left, 2 * NEG)
                    dve.drain()
                v.tensor_scalar(drop, left, 1.5 * NEG, NEG, ALU.is_gt, ALU.mult)
                dve.drain()
                v.tensor_tensor(tile(n), tile(n), drop, ALU.add)
                v.memset(thr[:, 0, n:n + 1], 0.5 * NEG)
                dve.drain()

            def exact(b, G):
                bank = Attn(b, "flag", G)
                bank.wait_full(dve)
                v.tensor_copy(flag_f[:, 0:16], bank.ps[0:1, 0:16]).then_inc(bank.free, 1)
                bank.wait_read(dve)
                v.tensor_reduce(flag_f[:, 16:20], flag_f[:, 0:16].rearrange("p (g i) -> p g i", i=4), AX.X, ALU.add)
                c1(v.tensor_reduce(flag_f[:, 20:21], flag_f[:, 0:16], AX.X, ALU.add))
                c1(v.tensor_copy(flag_i[:, :], flag_f[:, :]), apart=True)
                anywhere = dve.value_load(flag_i[0:1, 20:21])
                with dve.If(anywhere > 0):
                    for qg in range(LO, QG):
                        in_group = dve.value_load(flag_i[0:1, 16 + qg - LO:17 + qg - LO])
                        with dve.If(in_group > 0):
                            for n in range(4 * (qg - LO), 4 * (qg - LO) + 4):
                                here = dve.value_load(flag_i[0:1, n:n + 1])
                                with dve.If(here > 0):
                                    exact_tile(n)

            def lower_max(b, G, k):
                pb, n = lower_group(b, G, k)
                wait(dve, s_full, pb, 16, n + 1)
                c1(v.tensor_reduce(nmax[:, k, :], quad[:, :, 0:width(k)], AX.X, ALU.max, negate=True))
                v.tensor_scalar(bmax[:, k, :], nmax[:, k, :], SCALE, None, ALU.mult).then_inc(bmax_ready, 1)

            def lower_inverse(b, G, k):
                pb, n = lower_group(b, G, k)
                wait(dve, s_free, pb, 16, n + 1)
                v.reciprocal(rinv[:, k % 2, :], rsum[:, k % 2, :]).then_inc(p_ready, 1)

            def masked(b, G, qg):
                w = width(qg)
                wait(dve, e_ready, b, 8, 4 * G + qg - LO + 1)
                for i in range(4):
                    n = 4 * (qg - LO) + i
                    e = e_sb[:, qg % 2, i * w:(i + 1) * w]
                    ins = v.scalar_tensor_tensor(e, tile(n), thr[:, 0, n:n + 1], e, ALU.is_ge, ALU.mult,
                                                 accum_out=rsum[:, qg % 2, i:i + 1])
                c1(ins)
                v.reciprocal(rinv[:, qg % 2, :], rsum[:, qg % 2, :]).then_inc(p_ready, 1)

            def head_out(b, G, qg):
                turn = Attn(b, "o", G, qg)
                turn.wait_full(dve)
                c1(v.tensor_copy(o_scale[:, :], turn.ps[:, P:2 * P]))
                v.tensor_tensor(oT[:, 4 * G:4 * G + 4, 32 * qg:32 * qg + 32],
                                turn.ps[:, 0:P].rearrange("p (r q) -> p r q", r=REP),
                                o_scale[:, :].rearrange("p (r q) -> p r q", r=REP), ALU.mult).then_inc(turn.free, 1)

            def residual(kind, b, db, t, h):
                if (t, h) == (0, 0):
                    wait(dve, xres_in, b - 1, 16, 16)
                turn = Dense(kind, b, "wo", -1, t, h)
                turn.wait_full(dve)
                xs = x1[:, t, h * 512:(h + 1) * 512]
                v.tensor_tensor(xs, turn.ps[:, :], xs, ALU.add).then_inc(turn.free, 1)
                if h:
                    turn.wait_read(dve)

            def sim(kind, b, db, t):
                turn = Dense(kind, b, "sim", -1, t)
                turn.wait_full(dve)
                c2(v.tensor_reduce(small[:, 0:1], turn.ps[:, 0:S], AX.X, ALU.max, negate=True))
                v.tensor_scalar(small[:, 1:2], small[:, 0:1], XSCALE, None, ALU.mult).then_inc(smax_ready, 1)
                turn.wait_read(dve)
                c2(v.reciprocal(small[:, 3:4], small[:, 2:3]))
                v.tensor_scalar(p2[:, t, :], p2[:, t, :], small[:, 3:4], None, ALU.mult).then_inc(p2_ready, 1)

            def context(kind, b, db, c):
                for h in range(2):
                    turn = Dense(kind, b, "ctx", -1, c, h)
                    turn.wait_full(dve)
                    xs = x1[:, c, h * 512:(h + 1) * 512]
                    v.tensor_tensor(xs, turn.ps[:, :], xs, ALU.add).then_inc(turn.free, 1)
                turn.wait_read(dve)

            def gate_pick(kind, b, db, t):
                turn = Dense(kind, b, "cent", -1, t)
                turn.wait_full(dve)
                c2(v.tensor_reduce(small[:, 0:1], turn.ps[:, 0:NC], AX.X, ALU.max, negate=True))
                v.tensor_scalar(small[:, 1:2], small[:, 0:1], 10.0, None, ALU.mult).then_inc(gmax_ready, 1)
                turn.wait_read(dve)
                c2(v.reciprocal(small[:, 3:4], small[:, 2:3]))
                c2(v.tensor_scalar(gate[:, 1, :], gate[:, 0, :], small[:, 3:4], 0.01, ALU.mult, ALU.is_gt))
                v.tensor_tensor(hits[:, :], hits[:, :], gate[:, 1, :], ALU.max)
                c2(v.tensor_reduce(picked[:, t:t + 1], gate[:, 1, :], AX.X, ALU.max))

            def dense_out(kind, b, db, t, h):
                wait(dve, x2_out, b - 1, 16 * NT, 16 * NT)
                turn = Dense(kind, b, "dense", -1, t, h)
                turn.wait_full(dve)
                xs = x1[:, t, h * 512:(h + 1) * 512]
                v.scalar_tensor_tensor(xs, turn.ps[:, :], picked[:, t:t + 1], xs, ALU.mult, ALU.add).then_inc(turn.free, 1)

            def residual_after(kind, b, db, t, h):
                if (t, h) != (0, 0):
                    residual(kind, b, db, t, h)

            table = dict(rot=rotary, ln1=first_norm, ln2=later_norm, wo=residual_after, sim=sim, ctx=context,
                         cent=gate_pick, dense=dense_out)

            def body(kind, b):
                c1.start(b)
                if kind != "first":
                    c2.start(b - 1)
                for G in range(NG):
                    lower_max(b, G, 0)
                    upper_setup(b, G)
                    if G == 0 and kind != "first":
                        residual(kind, b, -1, 0, 0)
                    first_threshold(b, G)
                    for k in range(LO):
                        if k:
                            lower_max(b, G, k)
                        between = {5: lambda: lower_inverse(b, G, k)}
                        if k:
                            between[7] = lambda: head_out(b, G, k - 1)
                        early = (G, k) == (1, LO - 1)
                        if early:
                            between[11] = lambda: pieces(table, kind, b, G, k)
                        count(k, between)
                        if k < COUNTS - 1:
                            update(k)
                        else:
                            select(b, G)
                        if not early:
                            pieces(table, kind, b, G, k)
                    head_out(b, G, LO - 1)
                    exact(b, G)
                    dve.sem_inc(exact_done, 1)
                    for qg in range(LO, QG):
                        masked(b, G, qg)
                        if qg > LO:
                            head_out(b, G, qg - 1)
                        pieces(table, kind, b, G, qg)
                    head_out(b, G, QG - 1)
                assert c1.k == CHAIN1, c1.k
                assert kind == "first" or c2.k == CHAIN2, c2.k

            for t in range(NT):
                ln1(0, t, Dense("pro", 0, "xT", 0, 0, 1) if t else None)
            for name, *args in PROLOGUE:
                if name == "rot":
                    rotary("pro", 0, *args)
            body("first", 0)
            with dve.Fori(1, B - 1) as b:
                body("loop", b)
            body("last", B - 1)
            c2.start(B - 1)
            residual("tail", B, -1, 0, 0)
            for G in range(NG):
                for k in range(QG):
                    pieces(table, "tail", B, G, k)
            dve.wait_ge(assign_in, 16)
            v.tensor_scalar(one_hot, assign_sb, cluster_id[0:NC, :], None, ALU.is_equal).then_inc(fin_sel, 1)
            dve.wait_ge(fin_pe, 1)
            v.tensor_scalar(small[0:NC, 0:1], quad[0:NC, 0, 0:1], 0.0, None, ALU.is_gt).then_inc(fin_step, 1)
            dve.wait_ge(fin_step, 1)
            v.tensor_scalar(e_sb[0:NC, 0, 0:P], ones[0:NC, :], small[0:NC, 0:1], None, ALU.mult).then_inc(cluster_ready, 1)
            dve.wait_ge(fin_pe, 2)
            v.tensor_copy(row_on, quad[:, 1:3, :])
            v.tensor_scalar(row_off, quad[:, 1:3, :], -1.0, 1.0, ALU.mult, ALU.add).then_inc(fin_step, 1)
            dve.wait_ge(fin_step, 2)
            v.tensor_reduce(flag_f[:, 0:1], row_off[0:1, :, :], AX.XY, ALU.add).then_inc(fin_step, 1)
            dve.wait_ge(fin_step, 3)
            v.tensor_copy(flag_i[:, 0:1], flag_f[:, 0:1]).then_inc(rows_ready, 1)

        @block.scalar
        def _(act):
            s = nc.scalar

            def copy_out(turn, dst, rows=P, cols=512):
                turn.wait_full(act)
                s.activation(dst, turn.ps[0:rows, 0:cols], ACT.Copy).then_inc(turn.free, 1)

            def x_T(kind, b, db, t):
                for h in range(2):
                    turn = Dense(kind, b, "xT", db, t, h)
                    turn.wait_full(act)
                    s.activation(xT[:, 4 * h:4 * h + 4, t * P:(t + 1) * P],
                                 turn.ps[:, :].rearrange("p (k n) -> p k n", k=4), ACT.Copy).then_inc(turn.free, 1)

            def raw_q(kind, b, db, G, n):
                turn = Dense(kind, b, "q", db, G, n)
                turn.wait_full(act)
                wait(act, qk_ready, b + db, 6, 3 * G + (1 if n else -1))
                s.activation(q_raw[:, (n + 1) % 2, :], turn.ps[:, :], ACT.Copy).then_inc(turn.free, 1)

            def raw_kv(kind, b, db, G):
                turn = Dense(kind, b, "kv", db, G)
                turn.wait_full(act)
                wait(act, qk_ready, b + db, 6, 3 * G)
                s.activation(q_raw[:, 0, 0:S], turn.ps[:, 0:S], ACT.Copy)
                s.activation(v_sb[:, :, 4 * G * HD:4 * (G + 1) * HD], turn.ps[:, S:2 * S].rearrange("p (t c) -> p t c", t=NT),
                             ACT.Copy).then_inc(turn.free, 1)

            def upper_store(b, G, qg):
                wait(act, p_ready, b, 16, 8 * (G - 1) + qg + 1)
                pb, n = upper_group(b, G, qg)
                wait(act, s_full, pb, 16, n + 1)
                s.activation(s_tiles(qg), quad[:, :, 0:width(qg)], ACT.Copy).then_inc(s_free, 1)

            def upper_stats(b, G, qg):
                pb, n = upper_group(b, G, qg)
                wait(act, s_free, pb, 16, n + 1)
                for n in range(4 * (qg - LO), 4 * (qg - LO) + 4):
                    m = 32 * qg
                    src = s_tiles(qg)[:, n % 4, 0:m]
                    for a, func in enumerate((ACT.Copy, ACT.Square)):
                        step_n = 32 * G + 2 * n + a
                        wait(act, s_stats, b, 32 * NG, step_n - 1)
                        s.activation(act_junk[:, step_n % 2, 0:m], src, func,
                                     accum_out=ssum[:, a, n:n + 1]).then_inc(s_stats, 1)

            def exps(b, G, qg):
                w = width(qg)
                wait(act, bmax_ready, b, 10, 5 * G + (2 if qg >= LO else 1 if qg == 0 else qg + 2))
                lower = qg < LO
                if lower:
                    pass
                elif qg == LO:
                    wait(act, exact_done, b, NG, G + 1)
                for i in range(4):
                    src = quad[:, i, 0:w] if lower else s_tiles(qg)[:, i, :]
                    dst = e_sb[:, qg % 2, i * w:(i + 1) * w]
                    if lower:
                        ins = s.activation(dst, src, ACT.Exp, bias=bmax[:, qg, i:i + 1], scale=SCALE,
                                           accum_out=rsum[:, qg % 2, i:i + 1])
                    else:
                        ins = s.activation(dst, src, ACT.Exp, bias=bmax[:, qg, i:i + 1], scale=SCALE)
                ins.then_inc(s_free if lower else e_ready, 1)

            def p_out(b, G, qg):
                for kb, rows in parts(qg):
                    copy_out(Attn(b, "pT", G, qg, kb), pT_sb[0:rows, kb, :], rows=rows)

            def n_T(kind, b, db, t, name="nT"):
                for h in range(2):
                    copy_out(Dense(kind, b, name, -1, t, h), nT[:, 4 * h:4 * h + 4, :].rearrange("p k n -> p (k n)"))

            def m_T(kind, b, db, t):
                n_T(kind, b, db, t, "mT")

            def sim(kind, b, db, t):
                wait(act, smax_ready, b - 1, NT, t + 1)
                turn = Dense(kind, b, "sim", -1, t)
                s.activation(p2[:, t, :], turn.ps[:, 0:S], ACT.Exp, bias=small[:, 1:2], scale=XSCALE,
                             accum_out=small[:, 2:3]).then_inc(turn.free, 1)

            def gate_exp(kind, b, db, t):
                wait(act, gmax_ready, b - 1, NT, t + 1)
                turn = Dense(kind, b, "cent", -1, t)
                s.activation(gate[:, 0, :], turn.ps[:, 0:NC], ACT.Exp, bias=small[:, 1:2], scale=10.0,
                             accum_out=small[:, 2:3]).then_inc(turn.free, 1)

            copies = dict(xT=x_T, q=raw_q, kv=raw_kv, nT=n_T, mT=m_T)
            softmaxes = dict(sim=sim, cent=gate_exp)

            def body(kind, b):
                for G in range(NG):
                    ahead = (b, 1) if G == 0 else (b + 1, 0) if kind != "last" else None
                    for k in range(LO):
                        exps(b, G, k)
                        pieces(copies, kind, b, G, k)
                        p_out(b, G, k)
                        pieces(softmaxes, kind, b, G, k)
                    for qg in range(LO, QG):
                        if qg == LO:
                            pieces(copies, kind, b, G, qg)
                            exps(b, G, qg)
                        if qg + 1 < QG:
                            exps(b, G, qg + 1)
                        if qg > LO:
                            pieces(copies, kind, b, G, qg)
                        p_out(b, G, qg)
                        pieces(softmaxes, kind, b, G, qg)
                        if ahead:
                            upper_store(*ahead, qg)
                            if qg > LO:
                                upper_stats(*ahead, qg - 1)
                    if ahead:
                        upper_stats(*ahead, QG - 1)

            for name, *args in PROLOGUE:
                if name in copies:
                    copies[name]("pro", 0, *args)
            for qg in range(LO, QG):
                upper_store(0, 0, qg)
            for qg in range(LO, QG):
                upper_stats(0, 0, qg)
            body("first", 0)
            with act.Fori(1, B - 1) as b:
                body("loop", b)
            body("last", B - 1)
            for G in range(NG):
                for k in range(QG):
                    pieces(copies, "tail", B, G, k)
                    pieces(softmaxes, "tail", B, G, k)

        @block.gpsimd
        def _(pool):
            g = nc.gpsimd

            def power(b, n, per, got, made):
                wait(pool, got, b, per, n + 1)
                g.tensor_tensor(rstd[:, :], veps[:, :], half[:, 16:17], ALU.pow).then_inc(made, 1)

            def first_norm(kind, b, db, t):
                power(b + db, t, NT, var1, rstd1)

            def later_norm(kind, b, db, n):
                power(b - 1, n, 2 * NT, var2, rstd2)

            def rotary(kind, b, db, G, m):
                turn = Dense(kind, b, "rot", db, G, m)
                turn.wait_full(pool)
                raw = q_raw[:, m % 2, :]
                if m:
                    g.tensor_tensor(raw.rearrange("p (a s) -> p a s", a=2), raw.rearrange("p (a s) -> p a s", a=2),
                                    cos_sin[:, 0:1, :].to_broadcast([P, 2, S]), ALU.mult).then_inc(q_cos_ready, 1)
                else:
                    g.tensor_tensor(raw[:, 0:S], raw[:, 0:S], cos_sin[:, 0, :], ALU.mult).then_inc(q_cos_ready, 1)
                wait(pool, q_cos_ready, b + db, 6, 3 * G + m + 1)
                turn.wait_read(pool)
                if m:
                    for a in range(2):
                        r = 2 * (m - 1) + a
                        ins = g.tensor_tensor(qT[:, G, :, r * 32:(r + 1) * 32], raw[:, a * S:(a + 1) * S].rearrange("p (g q) -> p g q", q=32),
                                              q_sin[:, a * S:(a + 1) * S].rearrange("p (g q) -> p g q", q=32), ALU.add)
                else:
                    ins = g.tensor_tensor(kT[:, G, :], raw[:, 0:S], q_sin[:, 0:S], ALU.add)
                ins.then_inc(qk_ready, 1)

            def spread_of(b, G):
                wait(pool, var_s, b, NG, G + 1)
                g.tensor_tensor(sd[:, :], tmp[:, 1, :], half[:, 0:16], ALU.pow).then_inc(sd_ready, 1)

            table = dict(rot=rotary, ln1=first_norm, ln2=later_norm)

            def body(kind, b):
                for G in range(NG):
                    if kind != "tail":
                        spread_of(b, G)
                    for k in range(QG):
                        pieces(table, kind, b, G, k)

            pool.wait_ge(tables_in, 64)
            pool.wait_ge(consts_ready, 1)
            for t in range(NT):
                first_norm("pro", 0, 0, t)
            for name, *args in PROLOGUE:
                if name == "rot":
                    rotary("pro", 0, *args)
            body("first", 0)
            with pool.Fori(1, B - 1) as b:
                body("loop", b)
            body("last", B - 1)
            body("tail", B)
            pool.wait_ge(x2_out, 32 * B)
            pool.wait_ge(o_out, 16 * NT * B)
            pool.wait_ge(rows_ready, 1)
            rows_off = pool.value_load(flag_i[0:1, 0:1])
            with pool.If(rows_off > 0):
                with pool.Fori(0, B * NT) as n:
                    pool.dma_start(fix_a, out.rearrange("b (t p) d -> (b t) p d", p=P)[n]).then_inc(fix_in, 16)
                    pool.dma_start(fix_b, x2_dram.rearrange("b (t p) d -> (b t) p d", p=P)[n]).then_inc(fix_in, 16)
                    pool.wait_ge(fix_in, 32 * n + 32)
                    g.tensor_tensor(fix_a, fix_a, wo_sb[:, 0, :], ALU.mult)
                    g.tensor_tensor(fix_b, fix_b, wo_sb[:, 1, :], ALU.mult).then_inc(fix_step, 1)
                    pool.wait_ge(fix_step, 2 * n + 1)
                    g.tensor_tensor(fix_a, fix_a, fix_b, ALU.add).then_inc(fix_step, 1)
                    pool.wait_ge(fix_step, 2 * n + 2)
                    settle(pool)
                    pool.dma_start(out.rearrange("b (t p) d -> (b t) p d", p=P)[n], fix_a).then_inc(fix_out, 16)
                    pool.wait_ge(fix_out, 16 * n + 16)


CHAIN1 = 302
CHAIN2 = 12


def kernel(**inputs):
    import statistics
    import numpy as np
    import concourse.bacc as bacc
    from concourse.bass_utils import run_bass_kernel_spmd

    order = np.array([HD * (REP * (4 * G + i) + r) + d for G in range(NG) for r in range(REP) for i in range(4) for d in range(HD)])
    wq, wk, wv = (np.asarray(inputs[f"L0_attn_W{c}"]) for c in "qkv")
    wqkv = np.ascontiguousarray(np.concatenate(
        [w for G in range(NG) for w in (wq[order[4 * P * G:4 * P * (G + 1)]], wk[P * G:P * (G + 1)], wv[P * G:P * (G + 1)])]).T)
    wo = np.ascontiguousarray(np.asarray(inputs["L0_attn_Wo"]).T[order])
    wf = np.ascontiguousarray(np.asarray(inputs["L0_ffn_weight"]).T)
    cent = np.ascontiguousarray(np.asarray(inputs["L0_ffn_centroids"]).T)
    ctx_kv = np.ascontiguousarray(inputs["ctx_4096"])
    ctx_t = np.ascontiguousarray(ctx_kv.transpose(0, 2, 1))
    assign = np.ascontiguousarray(np.broadcast_to(np.asarray(inputs["L0_ffn_assignments"]), (NC, D)))
    bias = np.ascontiguousarray(np.asarray(inputs["L0_ffn_bias"]).reshape(KT_, P).T)

    f32 = np.float32
    inv_freq = (f32(1.0) / np.power(f32(10000.0), np.arange(0, HD, 2, dtype=f32) / f32(HD))).astype(f32)
    angle = np.outer(np.arange(S, dtype=f32), inv_freq).astype(f32)
    channel = np.arange(P) % (HD // 2)
    tables = np.ascontiguousarray(np.stack([np.cos(angle).T[channel], np.sin(angle).T[channel]], axis=1).astype(f32))
    masks = np.zeros((P, 3 * P + 32), f32)
    row = np.arange(P)
    masks[row, row] = 1.0
    for m in range(P):
        if m % HD < HD // 2:
            masks[m + HD // 2, P + m] = -1.0
        else:
            masks[m - HD // 2, P + m] = 1.0
        masks[m, 2 * P + np.arange(REP) * 32 + m % 32] = 1.0
        masks[m, 3 * P + m % 32 + 1:] = NEG
    probe = np.zeros((P, 3 * 16 + 16 * WIN + 1), f32)
    normal = statistics.NormalDist()
    for n in range(16):
        qg = LO + n // 4
        for p in range(P):
            keys = 32 * qg + p % 32 + 1
            z = normal.inv_cdf(1 - TARGET / keys)
            probe[p, n] = z
            probe[p, 16 + n] = DAMP / (keys * normal.pdf(z))
            probe[p, 32 + n] = 1 / (32 * qg)
        probe[:, 48 + n * WIN:48 + (n + 1) * WIN] = np.arange(WIN)
    probe[:, -1] = np.arange(P)

    arrays = dict(x=np.ascontiguousarray(inputs["x"]), ctx_kv=ctx_kv, ctx_t=ctx_t, wqkv=wqkv, wo=wo, wf=wf, cent=cent,
                  bias=bias, assign=assign, tables=tables, masks=masks, probe=probe)
    nc = bacc.Bacc("TRN2", target_bir_lowering=False, num_devices=1, dynamic_dma_scratch_size=2048)
    args = [nc.dram_tensor(f"in_{k}", a.shape, mybir.dt.from_np(a.dtype), kind="ExternalInput").ap() for k, a in arrays.items()]
    out = nc.dram_tensor("out_0", (B, S, D), F32, kind="ExternalOutput").ap()
    x2_dram = nc.dram_tensor("x2_dram", (B, S, D), F32).ap()
    build(nc, *args, out, x2_dram)
    got = run_bass_kernel_spmd(nc, [{f"in_{k}": a for k, a in arrays.items()}], core_ids=[0])
    return got.results[0]["out_0"]
```

```python
from contextlib import ExitStack

import concourse.bass as bass
from concourse import mybir

ALU = mybir.AluOpType
ACT = mybir.ActivationFunctionType
AX = mybir.AxisListType
F32 = mybir.dt.float32
I32 = mybir.dt.int32
BF16 = mybir.dt.bfloat16

P = 128
B, S, D = 8, 256, 1024
H, HKV, HD = 32, 8, 32
REP = H // HKV
KT_ = D // P
NT = S // P
NG = HKV // 4
WG = 6 * P
QG = S // 32
KEEP = 128
LO = KEEP // 32
NC = 64
SCALE = float(HD) ** -0.5
XSCALE = float(S) ** -0.5
EPS = 1e-5
NEG = -2.0 ** 100
EARLY = range(LO, QG - 1)
WIN = 8
TARGET = KEEP - (WIN - 1) / 2
RING = 3
COUNTS = 4
DAMP = 0.9


def width(qg):
    return 32 * (qg + 1)


HOFF = [0]
for _g in range(LO, QG):
    HOFF.append(HOFF[-1] + 4 * width(_g))


def attention_jobs():
    jobs = []
    for G in range(NG):
        for qg in range(LO):
            jobs += [("pT", G, qg, 0), ("o", G, qg)]
        jobs += [("flag", G), ("flag2", G)]
        for qg in range(LO, QG):
            jobs += [("pT", G, qg, 0), ("pT", G, qg, 1), ("o", G, qg)]
    assert len(jobs) % 2 == 0
    return jobs


STEPS = {
    (0, 0): [("wo", -1, 0, 0), ("wo", -1, 0, 1)],
    (0, 1): [("wo", -1, 1, 0), ("wo", -1, 1, 1), ("ln2", -1, 0)],
    (0, 2): [("kv", 0, 1), ("nT", -1, 0), ("sim", -1, 0), ("rot", 0, 1, 0), ("ln2", -1, 1)],
    (0, 3): [("q", 0, 1, 0), ("nT", -1, 1), ("q", 0, 1, 1), ("rot", 0, 1, 1), ("sim", -1, 1), ("rot", 0, 1, 2)],
    (0, 4): [("flag", 0, 0), ("ctx", -1, 0)],
    (0, 5): [("ctx", -1, 1), ("ln1", 1, 0)],
    (0, 6): [("xT", 1, 0), ("ln1", 1, 1)],
    (0, 7): [("xT", 1, 1), ("ln2", -1, 2)],
    (1, 0): [("kv", 1, 0), ("mT", -1, 0), ("q", 1, 0, 0), ("rot", 1, 0, 0), ("cent", -1, 0)],
    (1, 1): [("rot", 1, 0, 1), ("q", 1, 0, 1)],
    (1, 2): [("rot", 1, 0, 2), ("dense", -1, 0, 0), ("ln2", -1, 3)],
    (1, 3): [("dense", -1, 0, 1), ("mT", -1, 1), ("cent", -1, 1), ("dense", -1, 1, 0)],
    (1, 4): [("flag", 0, 1), ("dense", -1, 1, 1)],
}
PROLOGUE = [("xT", 0, 0), ("xT", 0, 1), ("kv", 0, 0), ("rot", 0, 0, 0), ("q", 0, 0, 0), ("rot", 0, 0, 1), ("q", 0, 0, 1), ("rot", 0, 0, 2)]

TAIL = [("wo", -1, 0, 0), ("wo", -1, 0, 1), ("ln2", -1, 0), ("wo", -1, 1, 0), ("nT", -1, 0), ("wo", -1, 1, 1), ("ln2", -1, 1),
        ("sim", -1, 0), ("nT", -1, 1), ("sim", -1, 1), ("ctx", -1, 0), ("ln2", -1, 2), ("ctx", -1, 1), ("mT", -1, 0), ("ln2", -1, 3),
        ("cent", -1, 0), ("dense", -1, 0, 0), ("dense", -1, 0, 1), ("mT", -1, 1), ("cent", -1, 1), ("dense", -1, 1, 0), ("dense", -1, 1, 1)]


def steps_of(kind, G, k):
    if kind == "tail":
        return TAIL if (G, k) == (0, 0) else []
    batches = {"first": (0, 1), "loop": (-1, 0, 1), "last": (-1, 0)}[kind]
    return [piece for piece in STEPS.get((G, k), []) if piece[1] in batches]


def dense_jobs(pieces):
    jobs = []
    for piece in pieces:
        if piece[0] in ("xT", "nT", "mT", "ctx"):
            jobs += [piece + (h,) for h in range(2)]
        elif piece[0] not in ("ln1", "ln2", "flag"):
            jobs.append(piece)
    return jobs


def build(nc, x, ctx_kv, ctx_t, wqkv, wo, wf, cent, bias, assign, tables, masks, probe, out, x2_dram):
    with ExitStack() as st:
        def sb(name, shape, dt=F32):
            return st.enter_context(nc.sbuf_tensor(name, shape, dt))

        def sem(name):
            return st.enter_context(nc.semaphore(name))

        wqkv_sb = sb("wqkv_sb", [P, KT_, D + 2 * HKV * HD])
        wo_sb = sb("wo_sb", [P, KT_, D])
        wf_sb = sb("wf_sb", [P, KT_, D])
        cent_sb = sb("cent_sb", [P, KT_, NC])
        cos_sin = sb("cos_sin", [P, 2, S])
        mask_sb = sb("mask_sb", [P, 3 * P + 32])
        ident, rotate, spread = (mask_sb[:, j * P:(j + 1) * P] for j in range(3))
        future = mask_sb[:, 3 * P:3 * P + 32]
        row_sb = sb("row_sb", [P, 3 * 16 + 16 * WIN + 1])
        probe_sb = row_sb[:, 0:48].rearrange("p (a n) -> p a n", a=3)
        iota8 = row_sb[:, 48:48 + 16 * WIN].rearrange("p (a n) -> p a n", a=16)
        cluster_id = row_sb[:, 48 + 16 * WIN:]
        ones = sb("ones", [P, P])
        bias_sb = sb("bias_sb", [P, KT_])
        half = sb("half", [P, 32])
        x_sb = sb("x_sb", [P, NT, D])
        e_sb = sb("e_sb", [P, 2, 4 * S])
        pT_sb = sb("pT_sb", [P, 2, 4 * P])
        xn = sb("xn", [P, D])
        xT = sb("xT", [P, KT_, S])
        oT = sb("oT", [P, KT_, S])
        qT = sb("qT", [P, NG, QG, REP * 32])
        kT = sb("kT", [P, NG, S])
        v_sb = sb("v_sb", [P, NT, HKV * HD])
        q_raw = sb("q_raw", [P, 2, 2 * S])
        q_sin = sb("q_sin", [P, 2 * S])
        below = sb("below", [P, RING, S])
        s_sb = sb("s_sb", [P, HOFF[-1]])
        hit = sb("hit", [P, RING, S], BF16)
        act_junk = sb("act_junk", [P, 2, S], BF16)
        o_scale = sb("o_scale", [P, P])
        rsum = sb("rsum", [P, 2, 4])
        rinv = sb("rinv", [P, 2, 4])
        ssum = sb("ssum", [P, 2, 16])
        nmax = sb("nmax", [P, QG, 4])
        bmax = sb("bmax", [P, QG, 4])
        tq = sb("tq", [P, 2, 16])
        dq = sb("dq", [P, 2, 16])
        sd = sb("sd", [P, 16])
        step = sb("step", [P, 4, 16])
        tmp = sb("tmp", [P, 4, 16])
        cand = sb("cand", [P, 16, WIN + 1])
        pick, prod = (below[:, j, 0:16 * WIN].rearrange("p (a n) -> p a n", a=16) for j in range(2))
        thr = sb("thr", [P, 2, 16])
        fail = sb("fail", [P, 16])
        flag_f = sb("flag_f", [1, 21])
        flag_i = sb("flag_i", [1, 21], I32)
        top8 = sb("top8", [P, 8])
        stats = sb("stats", [P, 12])
        mv = sb("mv", [P, 2])
        rstd = sb("rstd", [P, 1])
        veps = sb("veps", [P, 1])
        x1 = sb("x1", [P, NT, D])
        nT = sb("nT", [P, KT_, P])
        ctx_sb = sb("ctx_sb", [P, NT * D])
        ctxT_sb = ctx_sb[:, :].rearrange("p (k s) -> p k s", k=KT_)
        ctxv_sb = ctx_sb[:, :].rearrange("p (t d) -> p t d", t=NT)
        p2 = sb("p2", [P, NT, S])
        small = sb("small", [P, 4])
        picked = sb("picked", [P, NT])
        gate = sb("gate", [P, 2, NC])
        hits = sb("hits", [P, NC])

        assign_sb = xT[0:NC, 0:4, :].rearrange("p k n -> p (k n)").bitcast(I32)
        one_hot = s_sb[0:NC, 0:D]
        row_on = wo_sb[:, 0, :].rearrange("p (h n) -> p h n", h=2)
        row_off = wo_sb[:, 1, :].rearrange("p (h n) -> p h n", h=2)
        fix_a, fix_b = wo_sb[:, 2, :], wo_sb[:, 3, :]

        quad = st.enter_context(nc.psum_tensor("quad", [P, 4, 512], F32))
        acc1 = [st.enter_context(nc.psum_tensor(f"acc1_{j}", [P, 512], F32)) for j in range(2)]
        acc2 = [st.enter_context(nc.psum_tensor(f"acc2_{j}", [P, 512], F32)) for j in range(2)]

        tables_in, wqkv_in, wo_in, wf_in, consts_ready = map(sem, ("tables_in", "wqkv_in", "wo_in", "wf_in", "consts_ready"))
        x_in, xres_in, ctxT_in, ctxv_in = map(sem, ("x_in", "xres_in", "ctxT_in", "ctxv_in"))
        full1 = [sem(f"full1_{j}") for j in range(2)]
        free1 = [sem(f"free1_{j}") for j in range(2)]
        full2 = [sem(f"full2_{j}") for j in range(2)]
        free2 = [sem(f"free2_{j}") for j in range(2)]
        var1, rstd1, xn1, ln1_step = sem("var1"), sem("rstd1"), sem("xn1"), sem("ln1_step")
        var2, rstd2, xn2, ln2_step = sem("var2"), sem("rstd2"), sem("xn2"), sem("ln2_step")
        q_cos_ready, qk_ready = sem("q_cos_ready"), sem("qk_ready")
        s_full, s_free, s_stats = sem("s_full"), sem("s_free"), sem("s_stats")
        var_s, sd_ready = sem("var_s"), sem("sd_ready")
        bmax_ready, e_ready, p_ready, fail_ready, exact_done = map(
            sem, ("bmax_ready", "e_ready", "p_ready", "fail_ready", "exact_done"))
        x2_out, o_out, smax_ready, p2_ready, gmax_ready = map(
            sem, ("x2_out", "o_out", "smax_ready", "p2_ready", "gmax_ready"))
        fail2_ready, setup_step, wkv_in = sem("fail2_ready"), sem("setup_step"), sem("wkv_in")
        select_step, stage2_step = sem("select_step"), sem("stage2_step")
        passed = sem("passed")
        fin_sel, fin_pe, fin_step, rows_ready, fix_in, fix_step, fix_out, cluster_ready, assign_in = map(
            sem, ("fin_sel", "fin_pe", "fin_step", "rows_ready", "fix_in", "fix_step", "fix_out", "cluster_ready", "assign_in"))

        at1 = {j: (n % 2, n // 2) for n, j in enumerate(attention_jobs())}
        N1 = len(attention_jobs()) // 2
        pro = dense_jobs(PROLOGUE)
        seqs = {kind: [j for G in range(NG) for k in range(QG) for j in dense_jobs(steps_of(kind, G, k))]
                for kind in ("first", "loop", "last", "tail")}
        base_first = len(pro)
        base_loop = base_first + len(seqs["first"])
        N2 = len(seqs["loop"])
        base_last = base_loop + (B - 2) * N2
        base_tail = base_last + len(seqs["last"])
        assert base_loop % 2 == 0 and N2 % 2 == 0
        base = {"pro": 0, "first": base_first, "last": base_last, "tail": base_tail}
        seqs["pro"] = pro

        def wait(eng, s, b, per, k):
            v = b * per + k
            if isinstance(v, int) and v <= 0:
                return
            eng.wait_ge(s, v)

        def settle(eng):
            eng.sem_inc(passed, 1)

        class Turn:
            def wait_free(self, eng):
                wait(eng, self.free, self.b, self.per, self.n)

            def wait_read(self, eng):
                eng.wait_ge(self.free, (self.b) * self.per + self.n + 1)

            def wait_full(self, eng):
                eng.wait_ge(self.full, (self.b) * self.per + self.n + 1)

        class Attn(Turn):
            def __init__(self, b, *job):
                j, self.n = at1[job]
                self.b, self.per = b, N1
                self.ps, self.full, self.free = acc1[j], full1[j], free1[j]

        class Dense(Turn):
            def __init__(self, kind, b, *job):
                at = seqs[kind].index(job)
                if kind == "loop":
                    at += base_loop
                    self.b, self.per, self.n = b - 1, N2 // 2, at // 2
                else:
                    at += base[kind]
                    self.b, self.per, self.n = 0, 0, at // 2
                j = at % 2
                self.ps, self.full, self.free = acc2[j], full2[j], free2[j]

        def upper_group(b, G, qg):
            return b, 8 * G + qg - LO

        def lower_group(b, G, k):
            return b, 8 * G + LO + k

        def s_tiles(qg):
            o = HOFF[qg - LO]
            return s_sb[:, o:o + 4 * width(qg)].rearrange("p (i w) -> p i w", i=4)

        def parts(qg):
            w = width(qg)
            return [(0, min(w, P))] + ([(1, w - P)] if w > P else [])

        block = st.enter_context(nc.Block())

        def pieces(table, kind, b, G, k, part=slice(None)):
            for name, db, *args in steps_of(kind, G, k)[part]:
                if name in table:
                    table[name](kind, b, db, *args)

        @block.sync
        def _(sp):
            def load_x(b):
                wait(sp, xn1, b, NT, 0)
                sp.dma_start(x_sb[:, :, :], x[b].rearrange("(t p) d -> p t d", p=P)).then_inc(x_in, 16)

            def load_next(b):
                sp.dma_start(ctxT_sb, ctx_t[b].rearrange("(k p) s -> p k s", p=P)).then_inc(ctxT_in, 16)
                wait(sp, o_out, b, 16 * NT, 0)
                sp.dma_start(x1[:, :, :], x[b].rearrange("(t p) d -> p t d", p=P)).then_inc(xres_in, 16)

            def layers_of(kind, b, pb):
                Dense(kind, b, "sim", -1, NT - 1).wait_full(sp)
                sp.dma_start(ctxv_sb, ctx_kv[pb].rearrange("(t p) d -> p t d", p=P)).then_inc(ctxv_in, 16)
                for t in range(NT):
                    Dense(kind, b, "ctx", -1, t, 1).wait_read(sp)
                    sp.dma_start(x2_dram[pb, t * P:(t + 1) * P, :], x1[:, t, :]).then_inc(x2_out, 16)
                for t in range(NT):
                    Dense(kind, b, "dense", -1, t, 1).wait_read(sp)
                    sp.dma_start(out[pb, t * P:(t + 1) * P, :], x1[:, t, :]).then_inc(o_out, 16)

            wq_part = wqkv.rearrange("(k p) n -> p k n", p=P)
            sp.dma_start(row_sb[:, :], probe).then_inc(tables_in, 16)
            sp.dma_start(mask_sb[:, :], masks).then_inc(tables_in, 16)
            load_x(0)
            sp.dma_start(cos_sin[:, :, :], tables).then_inc(tables_in, 16)
            sp.dma_start(bias_sb[:, :], bias).then_inc(tables_in, 16)
            sp.dma_start(wqkv_sb[:, :, 4 * P:WG], wq_part[:, :, 4 * P:WG]).then_inc(wkv_in, 16)
            sp.dma_start(wqkv_sb[:, :, 0:4 * P], wq_part[:, :, 0:4 * P]).then_inc(wqkv_in, 16)
            sp.dma_start(wqkv_sb[:, :, WG:], wq_part[:, :, WG:]).then_inc(wqkv_in, 16)
            load_x(1)
            load_next(0)
            sp.dma_start(wo_sb[:, :, :], wo.rearrange("(k p) n -> p k n", p=P)).then_inc(wo_in, 16)
            sp.dma_start(cent_sb[:, :, :], cent.rearrange("(k p) n -> p k n", p=P)).then_inc(wf_in, 16)
            sp.dma_start(wf_sb[:, :, :], wf.rearrange("(k p) n -> p k n", p=P)).then_inc(wf_in, 16)
            with sp.Fori(1, B - 1) as b:
                load_x(b + 1)
                layers_of("loop", b, b - 1)
                load_next(b)
            layers_of("last", B - 1, B - 2)
            load_next(B - 1)
            Dense("last", B - 1, "kv", 0, 1).wait_full(sp)
            sp.dma_start(assign_sb, assign).then_inc(assign_in, 16)
            layers_of("tail", B, B - 1)
            sp.wait_ge(x2_out, 16 * NT * B)
            sp.wait_ge(o_out, 16 * NT * B)

        @block.tensor
        def _(pe):
            def begin(turn):
                turn.wait_free(pe)
                return turn

            def product(dst, lhs, rhs, steps=KT_):
                for k in range(steps):
                    mm = pe.matmul(dst, lhs(k), rhs(k), start=(k == 0), stop=(k == steps - 1))
                return mm

            def tile_T(turn, h):
                begin(turn)
                for j in range(4):
                    mm = pe.transpose(turn.ps[:, j * P:(j + 1) * P], xn[:, (4 * h + j) * P:(4 * h + j + 1) * P], ident)
                mm.then_inc(turn.full, 1)

            def x_T(kind, b, db, t):
                pe.wait_ge(xn1, (b + db) * NT + t + 1)
                for h in range(2):
                    tile_T(Dense(kind, b, "xT", db, t, h), h)

            def q_pair(kind, b, db, G, n):
                turn = begin(Dense(kind, b, "q", db, G, n))
                for a in range(2):
                    c = G * WG + (2 * n + a) * P
                    mm = product(turn.ps[:, a * S:(a + 1) * S], lambda k: wqkv_sb[:, k, c:c + P], lambda k: xT[:, k, :])
                mm.then_inc(turn.full, 1)

            def keys_values(kind, b, db, G):
                if G == 0:
                    Dense(kind, b, "xT", db, NT - 1, 1).wait_read(pe)
                c = G * WG + 4 * P
                turn = begin(Dense(kind, b, "kv", db, G))
                product(turn.ps[:, 0:S], lambda k: wqkv_sb[:, k, c:c + P], lambda k: xT[:, k, :])
                for t in range(NT):
                    mm = product(turn.ps[:, S + t * P:S + (t + 1) * P], lambda k: xT[:, k, t * P:(t + 1) * P],
                                 lambda k: wqkv_sb[:, k, c + P:c + 2 * P])
                mm.then_inc(turn.full, 1)

            def rot(kind, b, db, G, m):
                src = Dense(kind, b, "q", db, G, m - 1) if m else Dense(kind, b, "kv", db, G)
                src.wait_read(pe)
                cols = 2 * S if m else S
                turn = begin(Dense(kind, b, "rot", db, G, m))
                pe.matmul(turn.ps[:, 0:cols], rotate, q_raw[:, m % 2, 0:cols], start=True, stop=True).then_inc(turn.full, 1)

            def scores(group, G, qg):
                b, n = group
                wait(pe, s_free, b, 16, n)
                w = width(qg)
                for i in range(4):
                    r = slice(32 * i, 32 * i + 32)
                    pe.matmul(quad[:, i, 0:w], qT[r, G, qg, :], kT[r, G, 0:w], start=True, stop=False, skip_group_check=True)
                for i in range(4):
                    r = slice(32 * i, 32 * i + 32)
                    mm = pe.matmul(quad[:, i, w - 32:w], spread[r, :], future[r, :],
                                   start=False, stop=True, skip_group_check=True)
                mm.then_inc(s_full, 1)

            def upper_scores(b, G, qg):
                if qg == LO:
                    pe.wait_ge(qk_ready, b * 6 + 3 * G + 3)
                scores(upper_group(b, G, qg), G, qg)

            def weights_T(b, G, qg):
                w = width(qg)
                if qg < LO:
                    pb, n = lower_group(b, G, qg)
                    pe.wait_ge(s_free, pb * 16 + n + 1)
                else:
                    pe.wait_ge(p_ready, b * 16 + 8 * G + qg + 1)
                for kb, rows in parts(qg):
                    turn = begin(Attn(b, "pT", G, qg, kb))
                    if (qg, kb) == (LO, 1):
                        Attn(b, "flag2", G).wait_full(pe)
                    settle(pe)
                    for i in range(4):
                        o = i * w + kb * P
                        mm = pe.transpose(turn.ps[0:rows, i * P:(i + 1) * P], e_sb[:, qg % 2, o:o + rows], ident)
                    mm.then_inc(turn.full, 1)

            def values(b, G, qg):
                turn = begin(Attn(b, "o", G, qg))
                Attn(b, "pT", G, qg, len(parts(qg)) - 1).wait_read(pe)
                settle(pe)
                for i in range(4):
                    kv = 4 * G + i
                    for kb, rows in parts(qg):
                        pe.matmul(turn.ps[32 * i:32 * i + 32, 0:P], v_sb[0:rows, kb, kv * HD:(kv + 1) * HD],
                                  pT_sb[0:rows, kb, i * P:(i + 1) * P], start=(kb == 0), stop=True, skip_group_check=True)
                pe.wait_ge(p_ready, b * 16 + 8 * G + qg + 1)
                for i in range(4):
                    mm = pe.matmul(turn.ps[32 * i:32 * i + 32, P:2 * P], rinv[:, qg % 2, i:i + 1].to_broadcast([P, 32]),
                                   ident, start=False, stop=True, skip_group_check=True)
                mm.then_inc(turn.full, 1)

            def out_proj(kind, b, db, t, h):
                if h == 0:
                    Attn(b - 1, "o", NG - 1, LO - 1 if t == 0 else QG - 1).wait_read(pe)
                if kind == "loop" and (t, h) == (0, 0):
                    pe.wait_ge(wo_in, 16)
                turn = begin(Dense(kind, b, "wo", -1, t, h))
                product(turn.ps[:, :], lambda k: oT[:, k, t * P:(t + 1) * P],
                        lambda k: wo_sb[:, k, h * 512:(h + 1) * 512]).then_inc(turn.full, 1)

            def n_T(kind, b, db, t):
                pe.wait_ge(xn2, (b - 1) * 2 * NT + t + 1)
                for h in range(2):
                    tile_T(Dense(kind, b, "nT", -1, t, h), h)

            def m_T(kind, b, db, t):
                pe.wait_ge(xn2, (b - 1) * 2 * NT + NT + t + 1)
                for h in range(2):
                    tile_T(Dense(kind, b, "mT", -1, t, h), h)

            def sim(kind, b, db, t):
                Dense(kind, b, "nT", -1, t, 1).wait_read(pe)
                if t == 0:
                    pe.wait_ge(ctxT_in, (b - 1) * 16 + 16)
                turn = begin(Dense(kind, b, "sim", -1, t))
                product(turn.ps[:, 0:S], lambda k: nT[:, k, :], lambda k: ctxT_sb[:, k, :]).then_inc(turn.full, 1)

            def context(kind, b, db, c):
                if c == 0:
                    pe.wait_ge(p2_ready, (b - 1) * NT + NT)
                    pe.wait_ge(ctxv_in, (b - 1) * 16 + 16)
                for h in range(2):
                    turn = begin(Dense(kind, b, "ctx", -1, c, h))
                    product(turn.ps[:, :], lambda k: p2[:, k, c * P:(c + 1) * P],
                            lambda k: ctxv_sb[:, k, h * 512:(h + 1) * 512], NT).then_inc(turn.full, 1)

            def gate_logits(kind, b, db, t):
                if kind == "loop" and t == 0:
                    pe.wait_ge(wf_in, 32)
                Dense(kind, b, "mT", -1, t, 1).wait_read(pe)
                turn = begin(Dense(kind, b, "cent", -1, t))
                product(turn.ps[:, 0:NC], lambda k: nT[:, k, :], lambda k: cent_sb[:, k, :]).then_inc(turn.full, 1)

            def dense(kind, b, db, t, h):
                turn = begin(Dense(kind, b, "dense", -1, t, h))
                for j in range(4):
                    pe.matmul(turn.ps[:, j * P:(j + 1) * P], bias_sb[:, 4 * h + j:4 * h + j + 1].to_broadcast([P, P]),
                              ident, start=(j == 0), stop=False, skip_group_check=True)
                for k in range(KT_):
                    mm = pe.matmul(turn.ps[:, :], nT[:, k, :], wf_sb[:, k, h * 512:(h + 1) * 512],
                                   start=False, stop=(k == KT_ - 1), skip_group_check=True)
                mm.then_inc(turn.full, 1)

            def flags(kind, b, db, G, name="flag", ready=fail_ready):
                turn = begin(Attn(b, name, G))
                pe.wait_ge(ready, b * NG + G + 1)
                pe.matmul(turn.ps[0:1, 0:16], ones[:, 0:1], fail[:, :], start=True, stop=True).then_inc(turn.full, 1)

            table = dict(flag=flags, xT=x_T, q=q_pair, kv=keys_values, rot=rot, wo=out_proj, nT=n_T, mT=m_T, sim=sim,
                         ctx=context, cent=gate_logits, dense=dense)

            def body(kind, b):
                for G in range(NG):
                    scores(lower_group(b, G, 0), G, 0)
                    for k in range(LO):
                        pieces(table, kind, b, G, k)
                        weights_T(b, G, k)
                        if k + 1 < LO:
                            scores(lower_group(b, G, k + 1), G, k + 1)
                        values(b, G, k)
                    for qg in range(LO, QG):
                        pieces(table, kind, b, G, qg)
                        if qg == LO:
                            flags(kind, b, 0, G, "flag2", fail2_ready)
                        weights_T(b, G, qg)
                        if G == 0:
                            upper_scores(b, 1, qg)
                        elif kind != "last":
                            upper_scores(b + 1, 0, qg)
                        values(b, G, qg)

            pe.wait_ge(tables_in, 64)
            pe.wait_ge(consts_ready, 1)
            for name, *args in PROLOGUE:
                if name == "kv":
                    pe.wait_ge(wkv_in, 16)
                elif args == [0, 0, 0] and name == "q":
                    pe.wait_ge(wqkv_in, 32)
                table[name]("pro", 0, *args)
            for qg in range(LO, QG):
                upper_scores(0, 0, qg)
            body("first", 0)
            with pe.Fori(1, B - 1) as b:
                body("loop", b)
            body("last", B - 1)
            pieces(table, "tail", B, 0, 0)
            pe.wait_ge(fin_sel, 1)
            pe.matmul(quad[0:NC, 0, 0:1], hits[:, :], ones[:, 0:1], start=True, stop=True).then_inc(fin_pe, 1)
            pe.wait_ge(cluster_ready, 1)
            for h in range(2):
                mm = pe.matmul(quad[:, h + 1, :], e_sb[0:NC, 0, 0:P], one_hot[:, h * 512:(h + 1) * 512], start=True, stop=True)
            mm.then_inc(fin_pe, 1)

        @block.vector
        def _(dve):
            v = nc.vector

            class Chain:
                def __init__(self, s, per):
                    self.s, self.per, self.b, self.k = s, per, 0, 0

                def start(self, b, k=0):
                    self.b, self.k = b, k

                def put(self, ins):
                    self.k += 1
                    ins.then_inc(self.s, 1)
                    return self.k

                def upto(self, k, apart=False):
                    wait(dve, self.s, self.b, self.per, k)
                    if apart:
                        settle(dve)

                def __call__(self, ins, apart=False):
                    self.upto(self.put(ins), apart)

            c1, c2, ca = Chain(select_step, CHAIN1), Chain(stage2_step, CHAIN2), Chain(setup_step, 3 * NG)
            n1, n2 = Chain(ln1_step, 2 * NT), Chain(ln2_step, 4 * NT)

            v.memset(ones[:, :], 1.0)
            v.memset(hits[:, :], 0.0)
            v.memset(half[:, 0:16], 0.5)
            v.memset(half[:, 16:32], -0.5).then_inc(consts_ready, 1)
            dve.wait_ge(consts_ready, 1)
            dve.wait_ge(tables_in, 64)

            def layer_norm(b, n, per, src, link, var_sem, rstd_sem, xn_sem, xn_free):
                link.start(b, 2 * n)
                for h in range(2):
                    ins = v.bn_stats(stats[:, 6 * h:6 * h + 6], src[:, h * 512:(h + 1) * 512])
                link(ins, apart=True)
                link(v.bn_aggr(mv[:, :], stats[:, :]))
                v.tensor_scalar(veps[:, :], mv[:, 1:2], EPS, None, ALU.add).then_inc(var_sem, 1)
                if xn_free:
                    xn_free.wait_full(dve)
                dve.wait_ge(rstd_sem, b * per + n + 1)
                v.tensor_scalar(xn[:, :], src, mv[:, 0:1], rstd[:, 0:1], ALU.subtract, ALU.mult).then_inc(xn_sem, 1)

            def ln1(b, t, xn_free):
                if t == 0:
                    dve.wait_ge(x_in, b * 16 + 16)
                layer_norm(b, t, NT, x_sb[:, t, :], n1, var1, rstd1, xn1, xn_free)

            def ln2(b, n, xn_free):
                layer_norm(b, n, 2 * NT, x1[:, n % NT, :], n2, var2, rstd2, xn2, xn_free)

            def later_norm(kind, b, db, n):
                free = None
                if n % 2:
                    free = Dense(kind, b, "nT" if n < 2 else "mT", -1, 0, 1)
                elif n == 2:
                    free = Dense(kind, b, "xT", 1, NT - 1, 1) if kind == "loop" else Dense(kind, b, "nT", -1, 1, 1)
                ln2(b - 1, n, free)

            def first_norm(kind, b, db, t):
                if t:
                    free = Dense(kind, b, "xT", db, 0, 1)
                else:
                    free = Dense(kind, b, "nT", -1, 1, 1) if kind == "loop" else None
                ln1(b + db, t, free)

            def rotary(kind, b, db, G, m):
                turn = Dense(kind, b, "rot", db, G, m)
                turn.wait_full(dve)
                wait(dve, qk_ready, b + db, 6, 3 * G + m)
                if m:
                    v.tensor_tensor(q_sin[:, :].rearrange("p (a s) -> p a s", a=2), turn.ps[:, :].rearrange("p (a s) -> p a s", a=2),
                                    cos_sin[:, 1:2, :].to_broadcast([P, 2, S]), ALU.mult).then_inc(turn.free, 1)
                else:
                    v.tensor_tensor(q_sin[:, 0:S], turn.ps[:, 0:S], cos_sin[:, 1, :], ALU.mult).then_inc(turn.free, 1)

            def tile(n):
                return s_tiles(LO + n // 4)[:, n % 4, :]

            def row_maxima(b, G, groups):
                for qg in groups:
                    pb, n = upper_group(b, G, qg)
                    dve.wait_ge(s_free, pb * 16 + n + 1)
                    ins = v.tensor_reduce(nmax[:, qg, :], s_tiles(qg), AX.X, ALU.max, negate=True)
                return ins

            def row_variances(b, G, groups, link):
                c = slice(4 * (groups[0] - LO), 4 * (groups[-1] - LO) + 4)
                dve.wait_ge(s_stats, b * 32 * NG + 32 * G + 2 * c.stop)
                v.tensor_tensor(tmp[:, 0, c], ssum[:, 0, c], probe_sb[:, 2, c], ALU.mult)
                link(v.tensor_tensor(tmp[:, 1, c], ssum[:, 1, c], probe_sb[:, 2, c], ALU.mult))
                link(v.tensor_tensor(tmp[:, 2, c], tmp[:, 0, c], tmp[:, 0, c], ALU.mult))
                link(v.tensor_tensor(tmp[:, 1, c], tmp[:, 1, c], tmp[:, 2, c], ALU.subtract))
                v.tensor_scalar(tmp[:, 1, c], tmp[:, 1, c], 1e-30, None, ALU.max).then_inc(var_s, 1)

            def setup_ahead(b, G):
                ca.start(b, 3 * G)
                row_maxima(b, G, EARLY)
                row_variances(b, G, EARLY, ca)

            def setup_rest(b, G):
                c1(row_maxima(b, G, [QG - 1]))
                v.tensor_scalar(bmax[:, LO:, :], nmax[:, LO:, :], SCALE, None, ALU.mult).then_inc(bmax_ready, 1)
                row_variances(b, G, [QG - 1], c1)

            def first_threshold(b, G):
                dve.wait_ge(sd_ready, b * 2 * NG + 2 * G + 2)
                c1(v.tensor_tensor(tmp[:, 2, :], sd[:, :], probe_sb[:, 0, :], ALU.mult))
                v.tensor_tensor(tq[:, 0, :], tmp[:, 0, :], tmp[:, 2, :], ALU.add)
                c1(v.tensor_tensor(step[:, 0, :], sd[:, :], probe_sb[:, 1, :], ALU.mult))
                v.tensor_scalar(step[:, 1, :], step[:, 0, :], 4 / 9, None, ALU.mult)
                v.tensor_scalar(step[:, 3, :], step[:, 0, :], 2 / 9, None, ALU.mult)
                c1(v.tensor_scalar(step[:, 2, :], step[:, 0, :], 20 / 9, None, ALU.mult))

            def count(kind, b, G, k):
                new = k % 2
                counted, lowered, listed = [], [], []

                def count_tile(n):
                    w = width(LO + n // 4)
                    if n >= RING:
                        c1.upto((lowered if k == COUNTS - 1 else counted)[n - RING])
                    counted.append(c1.put(v.tensor_scalar(hit[:, n % RING, 0:w], tile(n), tq[:, new, n:n + 1], -TARGET,
                                                          ALU.is_ge, ALU.add, accum_out=dq[:, new, n:n + 1])))

                def lower_tile(n):
                    w = width(LO + n // 4)
                    c1.upto(max(counted[n], listed[n - RING] if n >= RING else 0))
                    lowered.append(c1.put(v.scalar_tensor_tensor(below[:, n % RING, 0:w], hit[:, n % RING, 0:w], NEG, tile(n),
                                                                 ALU.mult, ALU.add)))

                def list_tile(n):
                    w = width(LO + n // 4)
                    c1.upto(lowered[n], apart=True)
                    listed.append(c1.put(v.max(cand[:, n, 1:WIN + 1], below[:, n % RING, 0:w])))

                for n in range(16 + (2 if k == COUNTS - 1 else 0)):
                    if n == 4:
                        lower_inverse(b, G, k)
                    if n == 6 and k:
                        head_out(b, G, k - 1)
                    if n == 7 and (G, k) == (1, LO - 1):
                        pieces(table, kind, b, G, k, slice(0, 1))
                    if n < 16:
                        count_tile(n)
                    if k == COUNTS - 1:
                        if 1 <= n <= 16:
                            lower_tile(n - 1)
                        if n >= 2:
                            list_tile(n - 2)
                c1.upto(c1.k)

            def update(k, link=c1):
                new, old = k % 2, (k + 1) % 2
                t, d = tq[:, new, :], dq[:, new, :]
                slope = step[:, 0, :]
                if k:
                    slope = tmp[:, 0, :]
                    v.tensor_tensor(tmp[:, 1, :], dq[:, old, :], d, ALU.subtract)
                    link(v.tensor_tensor(tmp[:, 0, :], t, tq[:, old, :], ALU.subtract))
                    v.tensor_tensor(tmp[:, 0, :], tmp[:, 0, :], tmp[:, 1, :], ALU.mult)
                    link(v.tensor_tensor(tmp[:, 2, :], tmp[:, 1, :], tmp[:, 1, :], ALU.mult))
                    link(v.tensor_scalar(tmp[:, 2, :], tmp[:, 2, :], 1.0, None, ALU.max))
                    link(v.reciprocal(tmp[:, 1, :], tmp[:, 2, :]))
                    link(v.tensor_tensor(tmp[:, 2, :], tmp[:, 0, :], tmp[:, 1, :], ALU.mult))
                    link(v.tensor_tensor(tmp[:, 1, :], tmp[:, 2, :], step[:, 1 if k == 1 else 3, :], ALU.max))
                    v.tensor_tensor(tmp[:, 0, :], tmp[:, 1, :], step[:, 2, :], ALU.min)
                link(v.tensor_tensor(tmp[:, 3, :], d, d, ALU.mult))
                link(v.scalar_tensor_tensor(tmp[:, 3, :], tmp[:, 3, :], 13.0, d, ALU.is_gt, ALU.mult))
                link(v.tensor_tensor(tmp[:, 3, :], tmp[:, 3, :], slope, ALU.mult))
                link(v.tensor_tensor(tq[:, old, :], t, tmp[:, 3, :], ALU.add))

            def select(last, link, ready):
                v.tensor_copy(cand[:, :, 0:1], tq[:, last, :].rearrange("p (n o) -> p n o", o=1))
                link(v.tensor_scalar(tmp[:, 0, :], dq[:, last, :], -1.0, (WIN - 1) / 2, ALU.mult, ALU.add))
                link(v.tensor_tensor(pick[:, :, :], iota8[:, :, :],
                                     tmp[:, 0, :].rearrange("p (n o) -> p n o", o=1).to_broadcast([P, 16, WIN]), ALU.is_equal))
                for m in range(2):
                    link(v.tensor_tensor(prod[:, :, :], pick[:, :, :], cand[:, :, m:m + WIN], ALU.mult))
                    link(v.tensor_reduce(thr[:, m, :], prod[:, :, :], AX.X, ALU.add))
                v.tensor_tensor(fail[:, :], thr[:, 0, :], thr[:, 1, :], ALU.is_equal).then_inc(ready, 1)

            def exact_tile(n):
                w = width(LO + n // 4)
                left, drop = below[:, 0, 0:w], below[:, 1, 0:w]
                v.tensor_copy(left, tile(n))
                dve.drain()
                with dve.Fori(0, KEEP // 8) as _r:
                    v.max(top8[:, :], left)
                    dve.drain()
                    v.match_replace(left, top8[:, :], left, 2 * NEG)
                    dve.drain()
                v.tensor_scalar(drop, left, 1.5 * NEG, NEG, ALU.is_gt, ALU.mult)
                dve.drain()
                v.tensor_tensor(tile(n), tile(n), drop, ALU.add)
                v.memset(thr[:, 0, n:n + 1], 0.5 * NEG)
                dve.drain()

            def count_again(n):
                w = width(LO + n // 4)
                new = COUNTS % 2
                v.tensor_scalar(hit[:, 0, 0:w], tile(n), tq[:, new, n:n + 1], -TARGET, ALU.is_ge, ALU.add,
                                accum_out=dq[:, new, n:n + 1])
                dve.drain()
                v.scalar_tensor_tensor(below[:, 0, 0:w], hit[:, 0, 0:w], NEG, tile(n), ALU.mult, ALU.add)
                dve.drain()
                v.max(cand[:, n, 1:WIN + 1], below[:, 0, 0:w])
                dve.drain()

            def flagged_tiles(action):
                for qg in range(LO, QG):
                    in_group = dve.value_load(flag_i[0:1, 16 + qg - LO:17 + qg - LO])
                    with dve.If(in_group > 0):
                        for n in range(4 * (qg - LO), 4 * (qg - LO) + 4):
                            here = dve.value_load(flag_i[0:1, n:n + 1])
                            with dve.If(here > 0):
                                action(n)

            def exact(b, G):
                bank, bank2 = Attn(b, "flag", G), Attn(b, "flag2", G)
                bank.wait_full(dve)
                v.tensor_copy(flag_f[:, 0:16], bank.ps[0:1, 0:16]).then_inc(bank.free, 1)
                bank.wait_read(dve)
                v.tensor_reduce(flag_f[:, 16:20], flag_f[:, 0:16].rearrange("p (g i) -> p g i", i=4), AX.X, ALU.add)
                c1(v.tensor_reduce(flag_f[:, 20:21], flag_f[:, 0:16], AX.X, ALU.add))
                c1(v.tensor_copy(flag_i[:, :], flag_f[:, :]), apart=True)
                anywhere = dve.value_load(flag_i[0:1, 20:21])
                with dve.If(anywhere < 1):
                    dve.sem_inc(fail2_ready, 1)
                    dve.sem_inc(bank2.free, 1)
                with dve.If(anywhere > 0):
                    link = lambda ins: dve.drain()
                    update(COUNTS - 1, link)
                    link(v.tensor_copy(dq[:, COUNTS % 2, :], dq[:, (COUNTS - 1) % 2, :]))
                    flagged_tiles(count_again)
                    select(COUNTS % 2, link, fail2_ready)
                    bank2.wait_full(dve)
                    v.tensor_copy(flag_f[:, 0:16], bank2.ps[0:1, 0:16]).then_inc(bank2.free, 1)
                    dve.drain()
                    v.tensor_reduce(flag_f[:, 16:20], flag_f[:, 0:16].rearrange("p (g i) -> p g i", i=4), AX.X, ALU.add)
                    link(v.tensor_reduce(flag_f[:, 20:21], flag_f[:, 0:16], AX.X, ALU.add))
                    link(v.tensor_copy(flag_i[:, :], flag_f[:, :]))
                    left_over = dve.value_load(flag_i[0:1, 20:21])
                    with dve.If(left_over > 0):
                        flagged_tiles(exact_tile)

            def lower_max(b, G, k):
                pb, n = lower_group(b, G, k)
                dve.wait_ge(s_full, pb * 16 + n + 1)
                c1(v.tensor_reduce(nmax[:, k, :], quad[:, :, 0:width(k)], AX.X, ALU.max, negate=True))
                v.tensor_scalar(bmax[:, k, :], nmax[:, k, :], SCALE, None, ALU.mult).then_inc(bmax_ready, 1)

            def lower_inverse(b, G, k):
                pb, n = lower_group(b, G, k)
                dve.wait_ge(s_free, pb * 16 + n + 1)
                v.reciprocal(rinv[:, k % 2, :], rsum[:, k % 2, :]).then_inc(p_ready, 1)

            def masked(b, G, qg):
                w = width(qg)
                dve.wait_ge(e_ready, b * 8 + 4 * G + qg - LO + 1)
                for i in range(4):
                    n = 4 * (qg - LO) + i
                    e = e_sb[:, qg % 2, i * w:(i + 1) * w]
                    ins = v.scalar_tensor_tensor(e, tile(n), thr[:, 0, n:n + 1], e, ALU.is_ge, ALU.mult,
                                                 accum_out=rsum[:, qg % 2, i:i + 1])
                c1(ins)
                v.reciprocal(rinv[:, qg % 2, :], rsum[:, qg % 2, :]).then_inc(p_ready, 1)

            def head_out(b, G, qg):
                turn = Attn(b, "o", G, qg)
                turn.wait_full(dve)
                c1(v.tensor_copy(o_scale[:, :], turn.ps[:, P:2 * P]))
                v.tensor_tensor(oT[:, 4 * G:4 * G + 4, 32 * qg:32 * qg + 32],
                                turn.ps[:, 0:P].rearrange("p (r q) -> p r q", r=REP),
                                o_scale[:, :].rearrange("p (r q) -> p r q", r=REP), ALU.mult).then_inc(turn.free, 1)

            def residual(kind, b, db, t, h):
                if (t, h) == (0, 0):
                    dve.wait_ge(xres_in, (b - 1) * 16 + 16)
                turn = Dense(kind, b, "wo", -1, t, h)
                turn.wait_full(dve)
                xs = x1[:, t, h * 512:(h + 1) * 512]
                v.tensor_tensor(xs, turn.ps[:, :], xs, ALU.add).then_inc(turn.free, 1)
                if h:
                    turn.wait_read(dve)

            def sim(kind, b, db, t):
                turn = Dense(kind, b, "sim", -1, t)
                turn.wait_full(dve)
                c2(v.tensor_reduce(small[:, 0:1], turn.ps[:, 0:S], AX.X, ALU.max, negate=True))
                v.tensor_scalar(small[:, 1:2], small[:, 0:1], XSCALE, None, ALU.mult).then_inc(smax_ready, 1)
                turn.wait_read(dve)
                c2(v.reciprocal(small[:, 3:4], small[:, 2:3]))
                v.tensor_scalar(p2[:, t, :], p2[:, t, :], small[:, 3:4], None, ALU.mult).then_inc(p2_ready, 1)

            def context(kind, b, db, c):
                for h in range(2):
                    turn = Dense(kind, b, "ctx", -1, c, h)
                    turn.wait_full(dve)
                    xs = x1[:, c, h * 512:(h + 1) * 512]
                    v.tensor_tensor(xs, turn.ps[:, :], xs, ALU.add).then_inc(turn.free, 1)
                turn.wait_read(dve)

            def gate_pick(kind, b, db, t):
                turn = Dense(kind, b, "cent", -1, t)
                turn.wait_full(dve)
                c2(v.tensor_reduce(small[:, 0:1], turn.ps[:, 0:NC], AX.X, ALU.max, negate=True))
                v.tensor_scalar(small[:, 1:2], small[:, 0:1], 10.0, None, ALU.mult).then_inc(gmax_ready, 1)
                turn.wait_read(dve)
                c2(v.reciprocal(small[:, 3:4], small[:, 2:3]))
                c2(v.tensor_scalar(gate[:, 1, :], gate[:, 0, :], small[:, 3:4], 0.01, ALU.mult, ALU.is_gt))
                v.tensor_tensor(hits[:, :], hits[:, :], gate[:, 1, :], ALU.max)
                c2(v.tensor_reduce(picked[:, t:t + 1], gate[:, 1, :], AX.X, ALU.max))

            def dense_out(kind, b, db, t, h):
                dve.wait_ge(x2_out, (b - 1) * 16 * NT + 16 * NT)
                turn = Dense(kind, b, "dense", -1, t, h)
                turn.wait_full(dve)
                xs = x1[:, t, h * 512:(h + 1) * 512]
                v.scalar_tensor_tensor(xs, turn.ps[:, :], picked[:, t:t + 1], xs, ALU.mult, ALU.add).then_inc(turn.free, 1)

            table = dict(rot=rotary, ln1=first_norm, ln2=later_norm, wo=residual, sim=sim, ctx=context,
                         cent=gate_pick, dense=dense_out)

            def body(kind, b):
                c1.start(b)
                if kind != "first":
                    c2.start(b - 1)
                for G in range(NG):
                    lower_max(b, G, 0)
                    setup_rest(b, G)
                    first_threshold(b, G)
                    for k in range(LO):
                        if k:
                            lower_max(b, G, k)
                        count(kind, b, G, k)
                        if k < COUNTS - 1:
                            update(k)
                        else:
                            select((COUNTS - 1) % 2, c1, fail_ready)
                        pieces(table, kind, b, G, k, slice(1 if (G, k) == (1, LO - 1) else 0, None))
                    head_out(b, G, LO - 1)
                    exact(b, G)
                    dve.sem_inc(exact_done, 1)
                    for qg in range(LO, QG):
                        masked(b, G, qg)
                        if qg > LO:
                            head_out(b, G, qg - 1)
                        pieces(table, kind, b, G, qg)
                    if G == 0:
                        setup_ahead(b, 1)
                    elif kind != "last":
                        setup_ahead(b + 1, 0)
                    head_out(b, G, QG - 1)
                assert c1.k == CHAIN1, c1.k
                assert kind == "first" or c2.k == CHAIN2, c2.k

            for t in range(NT):
                ln1(0, t, Dense("pro", 0, "xT", 0, 0, 1) if t else None)
            for name, *args in PROLOGUE:
                if name == "rot":
                    rotary("pro", 0, *args)
            setup_ahead(0, 0)
            body("first", 0)
            with dve.Fori(1, B - 1) as b:
                body("loop", b)
            body("last", B - 1)
            c2.start(B - 1)
            pieces(table, "tail", B, 0, 0)
            dve.wait_ge(assign_in, 16)
            v.tensor_scalar(one_hot, assign_sb, cluster_id[0:NC, :], None, ALU.is_equal).then_inc(fin_sel, 1)
            dve.wait_ge(fin_pe, 1)
            v.tensor_scalar(small[0:NC, 0:1], quad[0:NC, 0, 0:1], 0.0, None, ALU.is_gt).then_inc(fin_step, 1)
            dve.wait_ge(fin_step, 1)
            v.tensor_scalar(e_sb[0:NC, 0, 0:P], ones[0:NC, :], small[0:NC, 0:1], None, ALU.mult).then_inc(cluster_ready, 1)
            dve.wait_ge(fin_pe, 2)
            v.tensor_copy(row_on, quad[:, 1:3, :])
            v.tensor_scalar(row_off, quad[:, 1:3, :], -1.0, 1.0, ALU.mult, ALU.add).then_inc(fin_step, 1)
            dve.wait_ge(fin_step, 2)
            v.tensor_reduce(flag_f[:, 0:1], row_off[0:1, :, :], AX.XY, ALU.add).then_inc(fin_step, 1)
            dve.wait_ge(fin_step, 3)
            v.tensor_copy(flag_i[:, 0:1], flag_f[:, 0:1]).then_inc(rows_ready, 1)

        @block.scalar
        def _(act):
            s = nc.scalar

            def copy_out(turn, dst, rows=P, cols=512):
                turn.wait_full(act)
                s.activation(dst, turn.ps[0:rows, 0:cols], ACT.Copy).then_inc(turn.free, 1)

            def x_T(kind, b, db, t):
                for h in range(2):
                    turn = Dense(kind, b, "xT", db, t, h)
                    turn.wait_full(act)
                    s.activation(xT[:, 4 * h:4 * h + 4, t * P:(t + 1) * P],
                                 turn.ps[:, :].rearrange("p (k n) -> p k n", k=4), ACT.Copy).then_inc(turn.free, 1)

            def raw_q(kind, b, db, G, n):
                turn = Dense(kind, b, "q", db, G, n)
                turn.wait_full(act)
                wait(act, qk_ready, b + db, 6, 3 * G + (1 if n else -1))
                s.activation(q_raw[:, (n + 1) % 2, :], turn.ps[:, :], ACT.Copy).then_inc(turn.free, 1)

            def raw_kv(kind, b, db, G):
                turn = Dense(kind, b, "kv", db, G)
                turn.wait_full(act)
                wait(act, qk_ready, b + db, 6, 3 * G)
                s.activation(q_raw[:, 0, 0:S], turn.ps[:, 0:S], ACT.Copy)
                s.activation(v_sb[:, :, 4 * G * HD:4 * (G + 1) * HD], turn.ps[:, S:2 * S].rearrange("p (t c) -> p t c", t=NT),
                             ACT.Copy).then_inc(turn.free, 1)

            def upper_store(b, G, qg):
                wait(act, p_ready, b, 16, 8 * (G - 1) + qg + 1)
                pb, n = upper_group(b, G, qg)
                act.wait_ge(s_full, pb * 16 + n + 1)
                s.activation(s_tiles(qg), quad[:, :, 0:width(qg)], ACT.Copy).then_inc(s_free, 1)

            def upper_stats(b, G, qg):
                pb, n = upper_group(b, G, qg)
                act.wait_ge(s_free, pb * 16 + n + 1)
                for n in range(4 * (qg - LO), 4 * (qg - LO) + 4):
                    m = 32 * qg
                    src = s_tiles(qg)[:, n % 4, 0:m]
                    for a, func in enumerate((ACT.Copy, ACT.Square)):
                        step_n = 32 * G + 2 * n + a
                        wait(act, s_stats, b, 32 * NG, step_n - 1)
                        s.activation(act_junk[:, step_n % 2, 0:m], src, func,
                                     accum_out=ssum[:, a, n:n + 1]).then_inc(s_stats, 1)

            def exps(b, G, qg):
                w = width(qg)
                act.wait_ge(bmax_ready, b * 10 + 5 * G + (2 if qg >= LO else 1 if qg == 0 else qg + 2))
                lower = qg < LO
                if lower:
                    pass
                elif qg == LO:
                    act.wait_ge(exact_done, b * NG + G + 1)
                for i in range(4):
                    src = quad[:, i, 0:w] if lower else s_tiles(qg)[:, i, :]
                    dst = e_sb[:, qg % 2, i * w:(i + 1) * w]
                    if lower:
                        ins = s.activation(dst, src, ACT.Exp, bias=bmax[:, qg, i:i + 1], scale=SCALE,
                                           accum_out=rsum[:, qg % 2, i:i + 1])
                    else:
                        ins = s.activation(dst, src, ACT.Exp, bias=bmax[:, qg, i:i + 1], scale=SCALE)
                ins.then_inc(s_free if lower else e_ready, 1)

            def p_out(b, G, qg):
                for kb, rows in parts(qg):
                    copy_out(Attn(b, "pT", G, qg, kb), pT_sb[0:rows, kb, :], rows=rows)

            def n_T(kind, b, db, t, name="nT"):
                for h in range(2):
                    copy_out(Dense(kind, b, name, -1, t, h), nT[:, 4 * h:4 * h + 4, :].rearrange("p k n -> p (k n)"))

            def m_T(kind, b, db, t):
                n_T(kind, b, db, t, "mT")

            def sim(kind, b, db, t):
                act.wait_ge(smax_ready, (b - 1) * NT + t + 1)
                turn = Dense(kind, b, "sim", -1, t)
                s.activation(p2[:, t, :], turn.ps[:, 0:S], ACT.Exp, bias=small[:, 1:2], scale=XSCALE,
                             accum_out=small[:, 2:3]).then_inc(turn.free, 1)

            def gate_exp(kind, b, db, t):
                act.wait_ge(gmax_ready, (b - 1) * NT + t + 1)
                turn = Dense(kind, b, "cent", -1, t)
                s.activation(gate[:, 0, :], turn.ps[:, 0:NC], ACT.Exp, bias=small[:, 1:2], scale=10.0,
                             accum_out=small[:, 2:3]).then_inc(turn.free, 1)

            copies = dict(xT=x_T, q=raw_q, kv=raw_kv, nT=n_T, mT=m_T)
            softmaxes = dict(sim=sim, cent=gate_exp)

            def body(kind, b):
                for G in range(NG):
                    ahead = (b, 1) if G == 0 else (b + 1, 0) if kind != "last" else None
                    for k in range(LO):
                        exps(b, G, k)
                        pieces(copies, kind, b, G, k)
                        p_out(b, G, k)
                        pieces(softmaxes, kind, b, G, k)
                    for qg in range(LO, QG):
                        if qg == LO:
                            pieces(copies, kind, b, G, qg)
                            exps(b, G, qg)
                        if qg + 1 < QG:
                            exps(b, G, qg + 1)
                        if qg > LO:
                            pieces(copies, kind, b, G, qg)
                        p_out(b, G, qg)
                        pieces(softmaxes, kind, b, G, qg)
                        if ahead:
                            if qg > LO:
                                upper_stats(*ahead, qg - 1)
                            upper_store(*ahead, qg)
                    if ahead:
                        upper_stats(*ahead, QG - 1)

            for name, *args in PROLOGUE:
                if name in copies:
                    copies[name]("pro", 0, *args)
            for qg in range(LO, QG):
                upper_store(0, 0, qg)
            for qg in range(LO, QG):
                upper_stats(0, 0, qg)
            body("first", 0)
            with act.Fori(1, B - 1) as b:
                body("loop", b)
            body("last", B - 1)
            pieces({**copies, **softmaxes}, "tail", B, 0, 0)

        @block.gpsimd
        def _(pool):
            g = nc.gpsimd

            def power(b, n, per, got, made):
                pool.wait_ge(got, b * per + n + 1)
                g.tensor_tensor(rstd[:, :], veps[:, :], half[:, 16:17], ALU.pow).then_inc(made, 1)

            def first_norm(kind, b, db, t):
                power(b + db, t, NT, var1, rstd1)

            def later_norm(kind, b, db, n):
                power(b - 1, n, 2 * NT, var2, rstd2)

            def rotary(kind, b, db, G, m):
                turn = Dense(kind, b, "rot", db, G, m)
                turn.wait_full(pool)
                raw = q_raw[:, m % 2, :]
                if m:
                    g.tensor_tensor(raw.rearrange("p (a s) -> p a s", a=2), raw.rearrange("p (a s) -> p a s", a=2),
                                    cos_sin[:, 0:1, :].to_broadcast([P, 2, S]), ALU.mult).then_inc(q_cos_ready, 1)
                else:
                    g.tensor_tensor(raw[:, 0:S], raw[:, 0:S], cos_sin[:, 0, :], ALU.mult).then_inc(q_cos_ready, 1)
                pool.wait_ge(q_cos_ready, (b + db) * 6 + 3 * G + m + 1)
                turn.wait_read(pool)
                if m:
                    for a in range(2):
                        r = 2 * (m - 1) + a
                        ins = g.tensor_tensor(qT[:, G, :, r * 32:(r + 1) * 32], raw[:, a * S:(a + 1) * S].rearrange("p (g q) -> p g q", q=32),
                                              q_sin[:, a * S:(a + 1) * S].rearrange("p (g q) -> p g q", q=32), ALU.add)
                else:
                    ins = g.tensor_tensor(kT[:, G, :], raw[:, 0:S], q_sin[:, 0:S], ALU.add)
                ins.then_inc(qk_ready, 1)

            def spread_of(b, G, groups):
                c = slice(4 * (groups[0] - LO), 4 * (groups[-1] - LO) + 4)
                pool.wait_ge(var_s, b * 2 * NG + 2 * G + (1 if len(groups) > 1 else 2))
                g.tensor_tensor(sd[:, c], tmp[:, 1, c], half[:, c], ALU.pow).then_inc(sd_ready, 1)

            table = dict(rot=rotary, ln1=first_norm, ln2=later_norm)

            def body(kind, b):
                for G in range(NG):
                    spread_of(b, G, [QG - 1])
                    for k in range(QG):
                        pieces(table, kind, b, G, k)
                    if (kind, G) != ("last", 1):
                        spread_of(*((b, 1) if G == 0 else (b + 1, 0)), EARLY)

            pool.wait_ge(tables_in, 64)
            pool.wait_ge(consts_ready, 1)
            for t in range(NT):
                first_norm("pro", 0, 0, t)
            for name, *args in PROLOGUE:
                if name == "rot":
                    rotary("pro", 0, *args)
            spread_of(0, 0, EARLY)
            body("first", 0)
            with pool.Fori(1, B - 1) as b:
                body("loop", b)
            body("last", B - 1)
            pieces(table, "tail", B, 0, 0)
            pool.wait_ge(x2_out, 32 * B)
            pool.wait_ge(o_out, 16 * NT * B)
            pool.wait_ge(rows_ready, 1)
            rows_off = pool.value_load(flag_i[0:1, 0:1])
            with pool.If(rows_off > 0):
                with pool.Fori(0, B * NT) as n:
                    pool.dma_start(fix_a, out.rearrange("b (t p) d -> (b t) p d", p=P)[n]).then_inc(fix_in, 16)
                    pool.dma_start(fix_b, x2_dram.rearrange("b (t p) d -> (b t) p d", p=P)[n]).then_inc(fix_in, 16)
                    pool.wait_ge(fix_in, 32 * n + 32)
                    g.tensor_tensor(fix_a, fix_a, wo_sb[:, 0, :], ALU.mult)
                    g.tensor_tensor(fix_b, fix_b, wo_sb[:, 1, :], ALU.mult).then_inc(fix_step, 1)
                    pool.wait_ge(fix_step, 2 * n + 1)
                    g.tensor_tensor(fix_a, fix_a, fix_b, ALU.add).then_inc(fix_step, 1)
                    pool.wait_ge(fix_step, 2 * n + 2)
                    settle(pool)
                    pool.dma_start(out.rearrange("b (t p) d -> (b t) p d", p=P)[n], fix_a).then_inc(fix_out, 16)
                    pool.wait_ge(fix_out, 16 * n + 16)


CHAIN1 = 302
CHAIN2 = 12


def kernel(**inputs):
    import statistics
    import numpy as np
    import concourse.bacc as bacc
    from concourse.bass_utils import run_bass_kernel_spmd

    order = np.array([HD * (REP * (4 * G + i) + r) + d for G in range(NG) for r in range(REP) for i in range(4) for d in range(HD)])
    wq, wk, wv = (np.asarray(inputs[f"L0_attn_W{c}"]) for c in "qkv")
    wqkv = np.ascontiguousarray(np.concatenate(
        [w for G in range(NG) for w in (wq[order[4 * P * G:4 * P * (G + 1)]], wk[P * G:P * (G + 1)], wv[P * G:P * (G + 1)])]).T)
    wo = np.ascontiguousarray(np.asarray(inputs["L0_attn_Wo"]).T[order])
    wf = np.ascontiguousarray(np.asarray(inputs["L0_ffn_weight"]).T)
    cent = np.ascontiguousarray(np.asarray(inputs["L0_ffn_centroids"]).T)
    ctx_kv = np.ascontiguousarray(inputs["ctx_4096"])
    ctx_t = np.ascontiguousarray(ctx_kv.transpose(0, 2, 1))
    assign = np.ascontiguousarray(np.broadcast_to(np.asarray(inputs["L0_ffn_assignments"]), (NC, D)))
    bias = np.ascontiguousarray(np.asarray(inputs["L0_ffn_bias"]).reshape(KT_, P).T)

    f32 = np.float32
    inv_freq = (f32(1.0) / np.power(f32(10000.0), np.arange(0, HD, 2, dtype=f32) / f32(HD))).astype(f32)
    angle = np.outer(np.arange(S, dtype=f32), inv_freq).astype(f32)
    channel = np.arange(P) % (HD // 2)
    tables = np.ascontiguousarray(np.stack([np.cos(angle).T[channel], np.sin(angle).T[channel]], axis=1).astype(f32))
    masks = np.zeros((P, 3 * P + 32), f32)
    row = np.arange(P)
    masks[row, row] = 1.0
    for m in range(P):
        if m % HD < HD // 2:
            masks[m + HD // 2, P + m] = -1.0
        else:
            masks[m - HD // 2, P + m] = 1.0
        masks[m, 2 * P + np.arange(REP) * 32 + m % 32] = 1.0
        masks[m, 3 * P + m % 32 + 1:] = NEG
    probe = np.zeros((P, 3 * 16 + 16 * WIN + 1), f32)
    normal = statistics.NormalDist()
    for n in range(16):
        qg = LO + n // 4
        for p in range(P):
            keys = 32 * qg + p % 32 + 1
            z = normal.inv_cdf(1 - TARGET / keys)
            probe[p, n] = z
            probe[p, 16 + n] = DAMP / (keys * normal.pdf(z))
            probe[p, 32 + n] = 1 / (32 * qg)
        probe[:, 48 + n * WIN:48 + (n + 1) * WIN] = np.arange(WIN)
    probe[:, -1] = np.arange(P)

    arrays = dict(x=np.ascontiguousarray(inputs["x"]), ctx_kv=ctx_kv, ctx_t=ctx_t, wqkv=wqkv, wo=wo, wf=wf, cent=cent,
                  bias=bias, assign=assign, tables=tables, masks=masks, probe=probe)
    nc = bacc.Bacc("TRN2", target_bir_lowering=False, num_devices=1, dynamic_dma_scratch_size=2048)
    args = [nc.dram_tensor(f"in_{k}", a.shape, mybir.dt.from_np(a.dtype), kind="ExternalInput").ap() for k, a in arrays.items()]
    out = nc.dram_tensor("out_0", (B, S, D), F32, kind="ExternalOutput").ap()
    x2_dram = nc.dram_tensor("x2_dram", (B, S, D), F32).ap()
    build(nc, *args, out, x2_dram)
    got = run_bass_kernel_spmd(nc, [{f"in_{k}": a for k, a in arrays.items()}], core_ids=[0])
    return got.results[0]["out_0"]
```
